# Optimizing a Trainium2 kernel written in Bass

```python
import numpy as np
import jax
import jax.numpy as jnp

def _softmax(x, axis=-1):
    return jax.nn.softmax(x, axis=axis)

def _gelu(x):
    return jax.nn.gelu(x, approximate=True)

def _silu(x):
    return jax.nn.silu(x)

def _sigmoid(x):
    return jax.nn.sigmoid(x)

def _layernorm(x, axis=-1, eps=1e-05):
    m = jnp.mean(x, axis=axis, keepdims=True)
    v = jnp.var(x, axis=axis, keepdims=True)
    return (x - m) / jnp.sqrt(v + eps)

def _scatter_add(tgt, idx, src, axis=0):
    return tgt.at[idx].add(src)

def _segment_sum(src, seg, n):
    return jax.ops.segment_sum(src, seg, n)
kernel_name = 'mk_audio_tower_d1_tok_audfeat768_r4_106b0e'

def setup_inputs(seed: int=0):
    np.random.seed(seed)
    _w = jnp.asarray

    def _rec_inputs():
        import jax
        import jax.numpy as jnp
        _rk = jax.random.key(seed)
        x = 0.000106427 + 1.00001 * jax.random.normal(jax.random.fold_in(_rk, 1), (16, 750, 192), jnp.float32)
        return x
    x = _rec_inputs()

    def _L0_tok_setup():
        import jax, jax.numpy as jnp
        import numpy as np
        D_MODEL = 192
        SEGMENT_SIZE = 128
        DILATION_RATE = 2
        key = jax.random.key(seed)
        x = jax.random.normal(key, (4, 4096, D_MODEL), dtype=jnp.float32)
        return {'x': x}
    _L0_tok_all = _L0_tok_setup()
    _L0_tok_in = {k: v for k, v in _L0_tok_all.items() if k in ()}
    del _L0_tok_all

    def _L0_attn_setup():
        import jax, jax.numpy as jnp
        import numpy as np
        import math
        DIM = 192
        HEADS = 12
        HEAD_DIM = DIM // HEADS
        key = jax.random.key(seed)
        ks = jax.random.split(key, 9)
        s = 1.0 / math.sqrt(DIM)
        x = jax.random.normal(ks[0], (8, 1024, DIM), dtype=jnp.float32)
        Wq = jax.random.normal(ks[1], (DIM, DIM), dtype=jnp.float32) * s
        bq = jnp.zeros((DIM,), dtype=jnp.float32)
        Wk = jax.random.normal(ks[2], (DIM, DIM), dtype=jnp.float32) * s
        bk = jnp.zeros((DIM,), dtype=jnp.float32)
        Wv = jax.random.normal(ks[3], (DIM, DIM), dtype=jnp.float32) * s
        bv = jnp.zeros((DIM,), dtype=jnp.float32)
        Wp = jax.random.normal(ks[4], (DIM, DIM), dtype=jnp.float32) * s
        bp = jnp.zeros((DIM,), dtype=jnp.float32)
        return {'x': x, 'Wq': Wq, 'bq': bq, 'Wk': Wk, 'bk': bk, 'Wv': Wv, 'bv': bv, 'Wp': Wp, 'bp': bp}
    _L0_attn_all = _L0_attn_setup()
    _L0_attn_in = {k: v for k, v in _L0_attn_all.items() if k in ('Wq', 'bq', 'Wk', 'bk', 'Wv', 'bv', 'Wp', 'bp')}
    del _L0_attn_all

    def _L0_ffn_setup():
        import jax, jax.numpy as jnp
        import numpy as np
        DEPTH = 11

        def _fff_forward(inputs, weights_in, weights_out, depth=DEPTH):
            B, S, _ = inputs.shape
            n_nodes = weights_in.shape[0]
            max_index = n_nodes - 1
            all_logits = jnp.einsum('bsd,nd->bsn', inputs, weights_in)

            def step(prev_idx, _):
                sel = jnp.clip(prev_idx, 0, max_index)
                logits = jnp.take_along_axis(all_logits, sel[..., None], axis=-1)[..., 0]
                new_idx = jnp.clip(2 * sel + 1 + (logits > 0).astype(sel.dtype), 0, max_index)
                return (new_idx, (logits, new_idx))
            idx0 = jnp.zeros((B, S), dtype=jnp.int32)
            _, (logits_seq, idx_seq) = jax.lax.scan(step, idx0, None, length=depth - 1)
            logits = jnp.concatenate([jnp.zeros((1, B, S), all_logits.dtype), logits_seq], axis=0)
            node_idx = jnp.concatenate([idx0[None], idx_seq], axis=0)
            act = jax.nn.gelu(logits, approximate=False)
            onehot = jax.nn.one_hot(node_idx, n_nodes, dtype=act.dtype)
            coeff = jnp.einsum('dbs,dbsn->bsn', act, onehot)
            return jnp.einsum('bsn,nd->bsd', coeff, weights_out)
        key = jax.random.key(seed)
        k1, k2, k3 = jax.random.split(key, 3)
        B, S, D = (4, 1024, 192)
        n_nodes = 2 * DEPTH - 1
        return {'inputs': jax.random.normal(k1, (B, S, D), dtype=jnp.float32), 'weights_in': jax.random.normal(k2, (n_nodes, D), dtype=jnp.float32), 'weights_out': jax.random.normal(k3, (n_nodes, D), dtype=jnp.float32)}
    _L0_ffn_all = _L0_ffn_setup()
    _L0_ffn_in = {k: v for k, v in _L0_ffn_all.items() if k in ('weights_in', 'weights_out')}
    del _L0_ffn_all
    return {'x': x, 'L0_attn_Wq': _L0_attn_in['Wq'], 'L0_attn_bq': _L0_attn_in['bq'], 'L0_attn_Wk': _L0_attn_in['Wk'], 'L0_attn_bk': _L0_attn_in['bk'], 'L0_attn_Wv': _L0_attn_in['Wv'], 'L0_attn_bv': _L0_attn_in['bv'], 'L0_attn_Wp': _L0_attn_in['Wp'], 'L0_attn_bp': _L0_attn_in['bp'], 'L0_ffn_weights_in': _L0_ffn_in['weights_in'], 'L0_ffn_weights_out': _L0_ffn_in['weights_out']}

def reference(x, L0_attn_Wq, L0_attn_bq, L0_attn_Wk, L0_attn_bk, L0_attn_Wv, L0_attn_bv, L0_attn_Wp, L0_attn_bp, L0_ffn_weights_in, L0_ffn_weights_out):
    import jax
    import jax.numpy as jnp

    def _L0_tok_ref(x):
        import jax, jax.numpy as jnp
        import numpy as np
        D_MODEL = 192
        SEGMENT_SIZE = 128
        DILATION_RATE = 2
        B, S, D = x.shape
        pad = -S % SEGMENT_SIZE
        if pad:
            x = jnp.pad(x, ((0, 0), (0, pad), (0, 0)))
        xs = x.reshape(B, -1, SEGMENT_SIZE, D)[:, :, ::DILATION_RATE, :]
        scale = 1.0 / jnp.sqrt(jnp.asarray(D, dtype=x.dtype))
        scores = jnp.einsum('bnqd,bnkd->bnqk', xs, xs) * scale
        attn = jax.nn.softmax(scores, axis=-1)
        out = jnp.einsum('bnqk,bnkd->bnqd', attn, xs)
        return out.reshape(B, -1, D)

    def _L0_attn_ref(x, Wq, bq, Wk, bk, Wv, bv, Wp, bp):
        import jax, jax.numpy as jnp
        import numpy as np
        import math
        DIM = 192
        HEADS = 12
        HEAD_DIM = DIM // HEADS
        B, N, C = x.shape
        H, D = (HEADS, HEAD_DIM)
        q = (x @ Wq.T + bq).reshape(B, N, H, D).transpose(0, 2, 1, 3)
        k = (x @ Wk.T + bk).reshape(B, N, H, D).transpose(0, 2, 1, 3)
        v = (x @ Wv.T + bv).reshape(B, N, H, D).transpose(0, 2, 1, 3)
        q = jax.nn.softmax(q, axis=-1)
        k = jax.nn.softmax(k, axis=-2)
        kv = jnp.einsum('bhnd,bhne->bhde', k, v) / math.sqrt(D)
        out = jnp.einsum('bhnd,bhde->bhne', q, kv)
        out = out.transpose(0, 2, 1, 3).reshape(B, N, C)
        return out @ Wp.T + bp

    def _L0_ffn_ref(inputs, weights_in, weights_out):
        import jax, jax.numpy as jnp
        import numpy as np
        DEPTH = 11

        def _fff_forward(inputs, weights_in, weights_out, depth=DEPTH):
            B, S, _ = inputs.shape
            n_nodes = weights_in.shape[0]
            max_index = n_nodes - 1
            all_logits = jnp.einsum('bsd,nd->bsn', inputs, weights_in)

            def step(prev_idx, _):
                sel = jnp.clip(prev_idx, 0, max_index)
                logits = jnp.take_along_axis(all_logits, sel[..., None], axis=-1)[..., 0]
                new_idx = jnp.clip(2 * sel + 1 + (logits > 0).astype(sel.dtype), 0, max_index)
                return (new_idx, (logits, new_idx))
            idx0 = jnp.zeros((B, S), dtype=jnp.int32)
            _, (logits_seq, idx_seq) = jax.lax.scan(step, idx0, None, length=depth - 1)
            logits = jnp.concatenate([jnp.zeros((1, B, S), all_logits.dtype), logits_seq], axis=0)
            node_idx = jnp.concatenate([idx0[None], idx_seq], axis=0)
            act = jax.nn.gelu(logits, approximate=False)
            onehot = jax.nn.one_hot(node_idx, n_nodes, dtype=act.dtype)
            coeff = jnp.einsum('dbs,dbsn->bsn', act, onehot)
            return jnp.einsum('bsn,nd->bsd', coeff, weights_out)
        return _fff_forward(inputs, weights_in, weights_out)
    h = _L0_tok_ref(x)
    h = h + _L0_attn_ref(_layernorm(h, axis=-1), L0_attn_Wq, L0_attn_bq, L0_attn_Wk, L0_attn_bk, L0_attn_Wv, L0_attn_bv, L0_attn_Wp, L0_attn_bp)
    h = h + _L0_ffn_ref(_layernorm(h, axis=-1), L0_ffn_weights_in, L0_ffn_weights_out)
    return h

_drawn_inputs = setup_inputs


def setup_inputs(seed=0):
    import zlib

    import numpy as np

    out = dict(_drawn_inputs(seed))
    spreads = {'L0_attn_bq': (0.0, 1.837),
     'L0_attn_bk': (0.0, 2.0),
     'L0_attn_bv': (0.0, 0.1),
     'L0_attn_bp': (0.0, 0.1)}
    factors = {}
    for name, (base, spread) in spreads.items():
        noise = np.random.default_rng([zlib.crc32(name.encode()), seed]).standard_normal(out[name].shape)
        drawn = base * np.exp(spread * noise) if base else spread * noise
        out[name] = jnp.asarray(drawn.astype(out[name].dtype))
    for name, factor in factors.items():
        out[name] = (out[name] * factor).astype(out[name].dtype)
    return out
```

```python
import concourse.bass as bass
from concourse import mybir
from contextlib import ExitStack


def audio_tower_kernel(nc, x, Wq, bq, Wk, bk, Wv, bv, Wp, bp, W_in, W_out, out):
    F32, F32R = mybir.dt.float32, mybir.dt.float32r
    ALU = mybir.AluOpType
    ACT = mybir.ActivationFunctionType
    AX = mybir.AxisListType

    NBATCH, ROWS, D = x.shape
    SEGMENT, DILATION = 128, 2
    SEGTOK = SEGMENT // DILATION
    NTOK = -(-ROWS // SEGMENT) * SEGTOK
    P = 128
    NT = NTOK // P
    LAST = (ROWS - (NT - 1) * P * DILATION + DILATION - 1) // DILATION
    HD = 16
    HEADS = D // HD
    CH = D // 2
    GH = CH // HD
    NODES = W_in.shape[0]
    XD = D + NODES
    LEAVES = 32
    PAIRS = NBATCH // 2
    BANK = 512
    PAD = 256
    SCALE = float(D) ** -0.5
    EPS = 1e-5
    A0 = 128
    B0 = D - A0
    SETUP_LOADS = 22
    STEPS_AT_END = 5.0

    ctx = ExitStack()
    with ctx:
        def sb(name, shape, dt=F32):
            return ctx.enter_context(nc.sbuf_tensor(name, shape, dt))

        def sem(name):
            return ctx.enter_context(nc.semaphore(name))

        ident = sb("ident", [P, P])
        head_mask = sb("head_mask", [CH, CH])
        w_nat = sb("w_nat", [CH, 3, 2, 2 * A0])
        w_hi = sb("w_hi", [P, 2, 3 * D], F32R)
        w_lo = sb("w_lo", [P, 2, 3 * D], F32R)
        wp_nat = sb("wp_nat", [CH, 2, D])
        wp_ext = sb("wp_ext", [CH, 2, XD])
        w_in = sb("w_in", [NODES, D])
        w_in_sum = sb("w_in_sum", [NODES, 1])
        w_in_mean = sb("w_in_mean", [NODES, 1])
        w_in_c = sb("w_in_c", [NODES, D])
        router = sb("router", [CH, 2, NODES])
        bq_raw = sb("bq_raw", [64, D])
        bq_round = sb("bq_round", [64, D], F32R)
        bq_split = sb("bq_split", [64, D], F32R)
        ones_r = sb("ones_r", [64, P], F32R)
        bk_col = sb("bk_col", [CH, 2])
        bv_col = sb("bv_col", [CH, 2])
        bp_col = sb("bp_col", [CH, 2])
        bp_row = sb("bp_row", [1, XD])
        head_share = sb("head_share", [1, CH])
        bv_diag = sb("bv_diag", [CH, 2, CH])
        m_const = sb("m_const", [CH, 2, XD])
        w_out_raw = sb("w_out_raw", [P, D])
        w_out_round = sb("w_out_round", [P, D], F32R)
        w_out_split = sb("w_out_split", [P, D], F32R)
        minus_half = sb("minus_half", [P, NT])

        x_tok = [sb(f"x_tok{i}", [P, NT, XD + 1]) for i in range(2)]
        x_ch = sb("x_ch", [CH, 2, NT, P + NODES])
        s_max = sb("s_max", [P, NT])
        seg_p = sb("seg_p", [P, NT, SEGTOK])
        seg_pt = sb("seg_pt", [P, NT, P])
        seg_rz = sb("seg_rz", [P, NT])
        h_ext = [sb(f"h_ext{i}", [P, NT, XD]) for i in range(2)]
        stats1 = sb("stats1", [P, NT, 6])
        moments1 = sb("moments1", [P, NT, 2])
        var1 = sb("var1", [P, NT])
        rstd1 = sb("rstd1", [P, NT])
        y = sb("y", [P, NT, D])
        y_split = sb("y_split", [P, NT, 3 * P])
        yt = sb("yt", [P, 3, NT * P], F32R)
        k_max = sb("k_max", [CH, 2])
        k_neg = sb("k_neg", [CH, 2])
        k_shift = sb("k_shift", [CH, 2])
        k_exp = sb("k_exp", [CH, 2, NT * P])
        k_sum = sb("k_sum", [CH, 2])
        k_rsum = sb("k_rsum", [CH, 2])
        k_tok = sb("k_tok", [P, NT, D])
        v_tok = sb("v_tok", [P, NT, D])
        q_max = sb("q_max", [P, NT, HEADS])
        q_exp = sb("q_exp", [P, NT, D])
        q_sum = sb("q_sum", [P, NT, HEADS])
        q_rsum = sb("q_rsum", [P, NT, HEADS])
        q_norm = sb("q_norm", [P, NT, D])
        q_ch = sb("q_ch", [CH, 2, NT * P])
        kv = sb("kv", [CH, 2, CH])
        mix = sb("mix", [CH, 2, XD])
        h2_ext = [sb(f"h2_ext{i}", [P, NT, XD]) for i in range(2)]
        stats2 = sb("stats2", [P, NT, 6])
        moments2 = sb("moments2", [P, NT, 2])
        var2 = sb("var2", [P, NT])
        rstd2 = sb("rstd2", [P, NT])
        logits = sb("logits", [P, 2, NT, NODES])
        gelu = sb("gelu", [P, 2 * NT, NODES])
        reach = sb("reach", [P, 2 * NT, NODES])
        tail1 = sb("tail1", [P, 2 * NT])
        tail2 = sb("tail2", [P, 2 * NT])
        coef = sb("coef", [P, 2 * NT, LEAVES])
        coef_split = sb("coef_split", [P, 2 * NT, 4 * LEAVES])
        coef_t = sb("coef_t", [P, 2, NT * P], F32R)
        result = [sb(f"result{i}", [P, NT, D]) for i in range(2)]

        psum = ctx.enter_context(nc.psum_tensor("psum", [P, 8 * BANK], F32))

        def bank(b, n=1):
            return psum[:, b * BANK:(b + n) * BANK]

        def tiles_in(b, width):
            return bank(b, 2).rearrange("p (t c) -> p t c", c=PAD)[:, 0:NT, 0:width]

        yt_ps = [bank(c) for c in range(3)]
        x_ch_ps = [bank(6 + c) for c in range(2)]
        k_ps = [bank(3 + c) for c in range(2)]
        qv_ps = bank(5, 3).rearrange("p (t c) -> p t c", c=BANK)
        SW = P + NODES
        s_ps = bank(2)[:, 0:NT * SW].rearrange("p (t c) -> p t c", c=SW)
        coef_ps = [bank(c) for c in range(2)]
        k_tok_ps = tiles_in(3, D)
        seg_pt_ps = bank(0)[0:SEGTOK, 0:NT * P].rearrange("p (t c) -> p t c", c=P)
        kv_ps = bank(5)[0:CH, 0:2 * CH].rearrange("p (g c) -> p g c", c=CH)
        ffn_ps = tiles_in(6, D)
        h_ps = tiles_in(1, XD + 1)
        q_ch_ps = [bank(3 + c) for c in range(2)]
        mix_ps = bank(5)[0:CH, 0:2 * XD].rearrange("p (g c) -> p g c", c=XD)
        out_ps = tiles_in(6, XD)

        const_built, tiles_cleared = sem("const_built"), sem("tiles_cleared")
        weights_loaded, w_transposed, wp_transposed = sem("weights_loaded"), sem("w_transposed"), sem("wp_transposed")
        setup_dve, router_ready = sem("setup_dve"), sem("router_ready")
        router_t_done, wp_router_done, bp_router_done = sem("router_t_done"), sem("wp_router_done"), sem("bp_router_done")
        m_const_done, const_ready = sem("m_const_done"), sem("const_ready")
        x_loaded = [sem("x_loaded0"), sem("x_loaded1")]
        x_ch_done, x_ch_copied = sem("x_ch_done"), sem("x_ch_copied")
        s_done, s_max_done, x_router_copied, s_shifted = sem("s_done"), sem("s_max_done"), sem("x_router_copied"), sem("s_shifted")
        seg_exp_done, seg_pt_done, seg_pt_copied = sem("seg_exp_done"), sem("seg_pt_done"), sem("seg_pt_copied")
        h_done, seg_rz_done, h_copied = sem("h_done"), sem("seg_rz_done"), sem("h_copied")
        stats1_done, moments1_done, var1_done, rstd1_done = sem("stats1_done"), sem("moments1_done"), sem("var1_done"), sem("rstd1_done")
        y_done, y_high_done, y_split_done = sem("y_done"), sem("y_high_done"), sem("y_split_done")
        yt_done, yt_copied = sem("yt_done"), sem("yt_copied")
        k_done, k_max_done, k_neg_done, k_shift_done = sem("k_done"), sem("k_max_done"), sem("k_neg_done"), sem("k_shift_done")
        k_exp_done, k_tok_done, k_tok_copied, k_rsum_done = sem("k_exp_done"), sem("k_tok_done"), sem("k_tok_copied"), sem("k_rsum_done")
        qv_done, v_copied = sem("qv_done"), sem("v_copied")
        q_max_done, q_shifted, q_exp_done, q_sum_done, q_rsum_done, q_norm_done = (
            sem("q_max_done"), sem("q_shifted"), sem("q_exp_done"), sem("q_sum_done"), sem("q_rsum_done"), sem("q_norm_done"))
        q_ch_done, q_ch_copied = sem("q_ch_done"), sem("q_ch_copied")
        kv_done, kv_masked, mix_done, mix_ready = sem("kv_done"), sem("kv_masked"), sem("mix_done"), sem("mix_ready")
        out_done, h2_done = sem("out_done"), sem("h2_done")
        stats2_done, moments2_done, var2_done, rstd2_done, logits_done = (
            sem("stats2_done"), sem("moments2_done"), sem("var2_done"), sem("rstd2_done"), sem("logits_done"))
        gelu_done, tree_step, coef_done = sem("gelu_done"), sem("tree_step"), sem("coef_done")
        coef_t_done, coef_t_copied, ffn_done, result_done = sem("coef_t_done"), sem("coef_t_copied"), sem("ffn_done"), sem("result_done")
        wait_passed = sem("wait_passed")
        stored = [sem("stored0"), sem("stored1")]

        def wait(eng, semaphore, count):
            if not (isinstance(count, int) and count <= 0):
                eng.wait_ge(semaphore, count)

        def wait_first(eng, semaphore, count):
            eng.wait_ge(semaphore, count)
            eng.nop().then_inc(wait_passed, 1)

        def schedule(eng, slot, looped=PAIRS - 1):
            slot(None, (0, 0), None)
            slot((0, 0), (0, 1), None)
            slot((0, 1), (1, 0), None)
            with eng.Fori(1, looped) as j:
                slot((j, 0), (j, 1), j - 1)
                slot((j, 1), (j + 1, 0), None)
            for j in range(looped, PAIRS - 1):
                slot((j, 0), (j, 1), j - 1)
                slot((j, 1), (j + 1, 0), None)
            last = PAIRS - 1
            slot((last, 0), (last, 1), last - 1)
            slot((last, 1), None, None)
            slot(None, None, last)

        def number(batch):
            return 2 * batch[0] + batch[1]

        block = ctx.enter_context(nc.Block())

        @block.sync
        def _(sp):
            for m, w in enumerate((Wq, Wv, Wk)):
                rows = w.rearrange("(h o) i -> o h i", h=2)
                sp.dma_start(w_nat[:, m, :, 0:D], rows).then_inc(weights_loaded, 16)
                sp.dma_start(w_nat[:, m, :, D:2 * A0], rows[:, :, A0:D]).then_inc(weights_loaded, 16)
            sp.dma_start(wp_nat[:, :, :], Wp.rearrange("(h o) i -> o h i", h=2)).then_inc(weights_loaded, 16)
            sp.dma_start(w_in[:, :], W_in).then_inc(weights_loaded, 16)
            for col, b in ((bk_col, bk), (bv_col, bv), (bp_col, bp)):
                sp.dma_start(col[:, :], b.rearrange("(g c) -> c g", g=2),
                             allow_slow_non_contiguous=True).then_inc(weights_loaded, 16)
            sp.dma_start(bp_row[0:1, 0:D], bp.rearrange("(a c) -> a c", a=1)).then_inc(weights_loaded, 16)
            sp.wait_ge(tiles_cleared, 4)
            for part in (0, 32):
                sp.dma_start(bq_raw[part:part + 1, :], bq.rearrange("(a c) -> a c", a=1)).then_inc(weights_loaded, 16)
            first = NODES // 2
            for s in range(4):
                at = s * LEAVES
                sp.dma_start(w_out_raw[at:at + NODES - 1, :], W_out[1:NODES, :]).then_inc(weights_loaded, 16)
                sp.dma_start(w_out_raw[at + NODES - 1:at + NODES - 1 + NODES - first, :],
                             W_out[NODES - 1:NODES, :].to_broadcast([NODES - first, D])).then_inc(weights_loaded, 16)

            def load_x(batch):
                j, p = batch
                rows = x[bass.ds(number(batch), 1), :, :].rearrange("a r c -> (a r) c")
                whole = rows[0:(NT - 1) * P * DILATION, :].rearrange("(t q s) c -> q t s c", q=P, s=DILATION)
                sp.dma_start(x_tok[p][:, 0:NT - 1, 0:D], whole[:, :, 0, :]).then_inc(x_loaded[p], 16)
                rest = rows[(NT - 1) * P * DILATION:ROWS, :].rearrange("(q s) c -> q s c", s=DILATION)
                sp.dma_start(x_tok[p][0:LAST, NT - 1, 0:D], rest[:, 0, :]).then_inc(x_loaded[p], 16)

            load_x((0, 0))
            load_x((0, 1))

            def store(pair, p):
                sp.wait_ge(result_done, 2 * pair + p + 1)
                dst = out[bass.ds(2 * pair + p, 1), :, :].rearrange("a (t q) c -> q (a t) c", q=P)
                sp.dma_start(dst, result[p][:, :, :]).then_inc(stored[p], 16)

            def slot(b, n, pair):
                if pair is not None:
                    store(pair, 0)
                if n is not None and not (isinstance(n[0], int) and n[0] + 1 >= PAIRS):
                    sp.wait_ge(h_done, number(n) + 1)
                    load_x((n[0] + 1, n[1]))
                if pair is not None:
                    store(pair, 1)

            schedule(sp, slot, looped=PAIRS - 2)
            for p in range(2):
                sp.wait_ge(stored[p], 16 * PAIRS)


        @block.gpsimd
        def _(pool):
            nc.gpsimd.memset(x_tok[0][:, :, :], 0.0).then_inc(tiles_cleared, 1)
            nc.gpsimd.memset(x_tok[1][:, :, :], 0.0).then_inc(tiles_cleared, 1)
            nc.gpsimd.memset(bq_raw[:, :], 0.0).then_inc(tiles_cleared, 1)
            nc.gpsimd.memset(w_out_raw[:, :], 0.0).then_inc(tiles_cleared, 1)
            nc.gpsimd.memset(ident[:, :], 0.0).then_inc(const_built, 1)
            nc.gpsimd.memset(head_mask[:, :], float(HD) ** -0.5).then_inc(const_built, 1)
            pool.wait_ge(const_built, 2)
            nc.gpsimd.affine_select(out=ident[:, :], in_=ident[:, :], compare_op=ALU.not_equal, fill=1.0,
                                    base=0, pattern=[[-1, P]], channel_multiplier=1).then_inc(const_built, 1)
            heads = head_mask[:, :].rearrange("p (g c) -> p g c", c=HD)
            nc.gpsimd.affine_select(out=heads, in_=heads, compare_op=ALU.is_ge, fill=0.0, base=0,
                                    pattern=[[-HD, GH], [0, HD]], channel_multiplier=1).then_inc(const_built, 1)
            pool.wait_ge(const_built, 4)
            nc.gpsimd.affine_select(out=heads, in_=heads, compare_op=ALU.is_ge, fill=0.0, base=HD - 1,
                                    pattern=[[HD, GH], [0, HD]], channel_multiplier=-1).then_inc(const_built, 1)
            nc.gpsimd.memset(ones_r[:, :].bitcast(F32), 1.0).then_inc(const_built, 1)
            nc.gpsimd.memset(head_share[:, :], 1.0 / HEADS).then_inc(const_built, 1)
            nc.gpsimd.memset(minus_half[:, :], -0.5).then_inc(const_built, 1)
            nc.gpsimd.memset(coef[:, :, :], 0.0).then_inc(const_built, 1)
            nc.gpsimd.memset(seg_pt[:, :, :], 0.0).then_inc(const_built, 1)
            pool.wait_ge(const_built, 10)
            pool.wait_ge(x_loaded[0], 32)
            for i in range(2):
                nc.gpsimd.memset(x_tok[i][:, :, XD:XD + 1], 1.0).then_inc(const_built, 1)

            TREE_STEPS = 13
            HALF = NODES // 2
            flat_logits = logits[:, :, :, :].rearrange("p b t n -> p (b t) n")
            coef4 = coef_split[:, :, :].bitcast(F32R).rearrange("p t (s e l) -> p t s e l", e=2, l=LEAVES)
            coef4_f = coef_split[:, :, :].rearrange("p t (s e l) -> p t s e l", e=2, l=LEAVES)

            def tree(pair):
                base = TREE_STEPS * pair if isinstance(pair, int) else pair * TREE_STEPS

                def step(k, instruction):
                    instruction.then_inc(tree_step, 1)
                    wait_first(pool, tree_step, base + k)

                def twice(a):
                    return a.unsqueeze(3).to_broadcast([P, 2 * NT, a.shape[2], 2])

                child = reach[:, :, 1:NODES].rearrange("p t (n c) -> p t n c", c=2)
                wait_first(pool, logits_done, 2 * pair + 2)
                nc.gpsimd.tensor_scalar(child[:, :, :, 1], flat_logits[:, :, 0:HALF], 0.0, None, ALU.is_gt)
                step(1, nc.gpsimd.tensor_scalar(child[:, :, :, 0], flat_logits[:, :, 0:HALF], 0.0, None, ALU.is_le))
                for k, (lo, hi) in enumerate(((3, 7), (7, 15), (15, NODES))):
                    kids = reach[:, :, lo:hi].rearrange("p t (n c) -> p t n c", c=2)
                    step(2 + k, nc.gpsimd.tensor_tensor(kids, kids, twice(reach[:, :, (lo - 1) // 2:(hi - 1) // 2]), ALU.mult))
                pool.wait_ge(gelu_done, pair + 1)
                head = coef[:, :, 0:NODES - 1].rearrange("p t (n c) -> p t n c", c=2)
                step(5, nc.gpsimd.tensor_tensor(head, child, twice(gelu[:, :, 0:HALF]), ALU.mult))
                step(6, nc.gpsimd.tensor_tensor(tail1[:, :], reach[:, :, HALF], reach[:, :, 5], ALU.add))
                step(7, nc.gpsimd.tensor_tensor(tail2[:, :], tail1[:, :], reach[:, :, 6], ALU.add))
                step(8, nc.gpsimd.tensor_tensor(reach[:, :, NODES - 1], reach[:, :, NODES - 1], tail2[:, :], ALU.add))
                step(9, nc.gpsimd.tensor_tensor(coef[:, :, NODES - 1:NODES - 1 + NODES - HALF], reach[:, :, HALF:NODES],
                                                gelu[:, :, HALF:NODES], ALU.mult))
                step(10, nc.gpsimd.tensor_scalar(tail1[:, :], gelu[:, :, NODES - 1], STEPS_AT_END, None, ALU.mult))
                step(11, nc.gpsimd.tensor_tensor(coef[:, :, LEAVES - 2], coef[:, :, LEAVES - 2], tail1[:, :], ALU.add))
                whole = coef[:, :, :].unsqueeze(2).to_broadcast([P, 2 * NT, 2, LEAVES])
                step(12, nc.gpsimd.tensor_copy(coef4[:, :, :, 0, :], whole))
                step(13, nc.gpsimd.tensor_tensor(coef4[:, :, :, 1, :], whole, coef4_f[:, :, :, 0, :], ALU.subtract))
                nc.gpsimd.nop().then_inc(coef_done, 1)

            def slot(b, n, pair):
                if pair is not None:
                    tree(pair)
                if b is not None:
                    pool.wait_ge(q_rsum_done, number(b) + 1)
                    wait(pool, q_ch_done, 2 * number(b))
                    by_head = q_norm[:, :, :].rearrange("p t (h c) -> p t h c", c=HD)
                    nc.gpsimd.tensor_tensor(by_head, q_exp[:, :, :].rearrange("p t (h c) -> p t h c", c=HD),
                                            q_rsum[:, :, :].unsqueeze(3).to_broadcast([P, NT, HEADS, HD]),
                                            ALU.mult).then_inc(q_norm_done, 1)
                if n is not None:
                    wait_first(pool, moments1_done, NT * (number(n) + 1))
                    nc.gpsimd.tensor_scalar(var1[:, :], moments1[:, :, 1], EPS, None, ALU.add).then_inc(var1_done, 1)
                    pool.wait_ge(var1_done, number(n) + 1)
                    nc.gpsimd.tensor_tensor(rstd1[:, :], var1[:, :], minus_half[:, :], ALU.pow).then_inc(rstd1_done, 1)
                    wait(pool, yt_done, 3 * number(n))
                    wait_first(pool, y_done, NT * (number(n) + 1))
                    high = y_split[:, :, 0:D]
                    nc.gpsimd.tensor_copy(high.bitcast(F32R), y[:, :, :]).then_inc(y_high_done, 1)
                    pool.wait_ge(y_high_done, number(n) + 1)
                    nc.gpsimd.tensor_tensor(y_split[:, :, D:2 * A0].bitcast(F32R), y[:, :, A0:D],
                                            high[:, :, A0:D], ALU.subtract).then_inc(y_split_done, 1)
                    nc.gpsimd.tensor_tensor(y_split[:, :, 2 * A0:3 * P].bitcast(F32R), y[:, :, 0:A0],
                                            high[:, :, 0:A0], ALU.subtract).then_inc(y_split_done, 1)
                if b is not None:
                    wait_first(pool, moments2_done, NT * (number(b) + 1))
                    nc.gpsimd.tensor_scalar(var2[:, :], moments2[:, :, 1], EPS, None, ALU.add).then_inc(var2_done, 1)
                    pool.wait_ge(var2_done, number(b) + 1)
                    nc.gpsimd.tensor_tensor(rstd2[:, :], var2[:, :], minus_half[:, :], ALU.pow).then_inc(rstd2_done, 1)
                    pool.wait_ge(rstd2_done, number(b) + 1)
                    wait(pool, gelu_done, b[0])
                    nc.gpsimd.tensor_tensor(logits[:, b[1], :, :], h2_ext[b[1]][:, :, D:XD],
                                            rstd2[:, :].unsqueeze(2).to_broadcast([P, NT, NODES]),
                                            ALU.mult).then_inc(logits_done, 1)

            schedule(pool, slot)

        @block.scalar
        def _(act):
            def slot(b, n, pair):
                if pair is not None:
                    act.wait_ge(logits_done, 2 * pair + 2)
                    wait(act, coef_done, pair)
                    nc.scalar.activation(gelu[:, :, :], logits[:, :, :, :].rearrange("p b t n -> p (b t) n"),
                                         ACT.Gelu).then_inc(gelu_done, 1)
                if b is not None:
                    for c in range(3):
                        act.wait_ge(yt_done, 3 * number(b) + c + 1)
                        nc.scalar.activation(yt[:, c, :], yt_ps[c][:, 0:NT * P], ACT.Copy).then_inc(yt_copied, 1)
                if n is not None:
                    for c in range(2):
                        act.wait_ge(x_ch_done, 2 * number(n) + c + 1)
                        nc.scalar.activation(x_ch[:, c, :, 0:P],
                                             x_ch_ps[c][0:CH, 0:NT * P].rearrange("p (t c) -> p t c", c=P),
                                             ACT.Copy).then_inc(x_ch_copied, 1)
                if b is not None:
                    act.wait_ge(k_shift_done, number(b) + 1)
                    for g in range(2):
                        nc.scalar.activation(k_exp[:, g, :], k_ps[g][0:CH, 0:NT * P], ACT.Exp,
                                             bias=k_shift[:, g:g + 1],
                                             accum_out=k_sum[:, g:g + 1]).then_inc(k_exp_done, 1)
                    act.wait_ge(q_shifted, number(b) + 1)
                    nc.scalar.activation(q_exp[:, :, :], q_exp[:, :, :], ACT.Exp).then_inc(q_exp_done, 1)
                    nc.scalar.activation(v_tok[:, :, :], qv_ps[:, :, D:2 * D], ACT.Copy).then_inc(v_copied, 1)
                if pair is not None:
                    for i in range(2):
                        act.wait_ge(coef_t_done, 2 * pair + i + 1)
                        nc.scalar.activation(coef_t[:, i, :], coef_ps[i][:, 0:NT * P], ACT.Copy).then_inc(coef_t_copied, 1)
                if n is not None:
                    act.wait_ge(s_shifted, 2 * (number(n) + 1))
                    nc.scalar.activation(seg_p[:, :, :], seg_p[:, :, :], ACT.Exp, scale=SCALE).then_inc(seg_exp_done, 1)
                    act.wait_ge(seg_rz_done, number(n) + 1)
                    for t in range(NT):
                        nc.scalar.activation(h_ext[n[1]][:, t, :], h_ps[:, t, 0:XD], ACT.Copy,
                                             scale=seg_rz[:, t:t + 1]).then_inc(h_copied, 1)
                if b is not None:
                    for g in range(2):
                        act.wait_ge(q_ch_done, 2 * number(b) + g + 1)
                        nc.scalar.activation(q_ch[:, g, :], q_ch_ps[g][0:CH, 0:NT * P], ACT.Copy).then_inc(q_ch_copied, 1)

            schedule(act, slot)

        @block.vector
        def _(dve):
            steps = [0]

            def step(instruction):
                steps[0] += 1
                instruction.then_inc(setup_dve, 1)
                dve.wait_ge(setup_dve, steps[0])

            dve.wait_ge(weights_loaded, 16 * SETUP_LOADS)
            step(nc.vector.tensor_reduce(w_in_sum[:, :], w_in[:, :], AX.X, ALU.add))
            step(nc.vector.tensor_scalar(w_in_mean[:, :], w_in_sum[:, :], 1.0 / D, None, ALU.mult))
            nc.vector.tensor_scalar(w_in_c[:, :], w_in[:, :], w_in_mean[:, 0:1], None, ALU.subtract).then_inc(router_ready, 1)
            w_ps = bank(0, 3).rearrange("p (m c) -> p m c", c=BANK)[:, :, 0:2 * D].rearrange("p m (a o) -> p a m o", a=2)
            dve.wait_ge(w_transposed, 1)
            for a in range(2):
                nc_hi = w_hi[:, a, :].rearrange("p (m o) -> p m o", m=3)
                step(nc.vector.tensor_copy(nc_hi, w_ps[:, a]))
                step(nc.vector.tensor_tensor(w_lo[:, a, :].rearrange("p (m o) -> p m o", m=3), w_ps[:, a],
                                             nc_hi.bitcast(F32), ALU.subtract))
            dve.wait_ge(wp_transposed, 1)
            step(nc.vector.tensor_copy(wp_ext[:, :, 0:D], bank(3)[0:CH, 0:2 * D].rearrange("p (g c) -> p g c", g=2)))
            step(nc.vector.tensor_copy(bq_round[:, :], bq_raw[:, :]))
            step(nc.vector.tensor_copy(bq_split[0:32, :], bq_round[0:32, :].bitcast(F32)))
            step(nc.vector.tensor_tensor(bq_split[32:64, :], bq_raw[32:64, :], bq_round[32:64, :].bitcast(F32), ALU.subtract))
            step(nc.vector.tensor_copy(w_out_round[:, :], w_out_raw[:, :]))
            step(nc.vector.tensor_copy(w_out_split[0:64, :], w_out_round[0:64, :].bitcast(F32)))
            step(nc.vector.tensor_tensor(w_out_split[64:P, :], w_out_raw[64:P, :], w_out_round[64:P, :].bitcast(F32), ALU.subtract))
            dve.wait_ge(router_t_done, 1)
            router_ps = bank(4)[0:CH, 0:2 * NODES].rearrange("p (g n) -> p g n", g=2)
            nc.vector.tensor_copy(router[:, :, :], router_ps).then_inc(router_ready, 1)
            step(nc.vector.tensor_copy(x_ch[:, :, :, P:P + NODES],
                                       router_ps.unsqueeze(2).to_broadcast([CH, 2, NT, NODES])))
            dve.wait_ge(wp_router_done, 1)
            step(nc.vector.tensor_copy(wp_ext[:, :, D:XD], bank(5)[0:CH, 0:2 * NODES].rearrange("p (g n) -> p g n", g=2)))
            dve.wait_ge(bp_router_done, 1)
            step(nc.vector.tensor_copy(bp_row[0:1, D:XD], bank(6)[0:1, 0:NODES]))
            for g in range(2):
                step(nc.vector.tensor_scalar(bv_diag[:, g, :], head_mask[:, :], bv_col[:, g:g + 1], None, ALU.mult))
            nc.vector.tensor_copy(k_sum[:, :], bk_col[:, :]).then_inc(router_ready, 1)
            dve.wait_ge(m_const_done, 1)
            step(nc.vector.tensor_copy(m_const[:, :, :], bank(7)[0:CH, 0:2 * XD].rearrange("p (g c) -> p g c", g=2)))
            nc.vector.nop().then_inc(const_ready, 1)

            def by_head(a):
                return a.rearrange("p t (h c) -> p t h c", c=HD)

            def seg_half(s):
                return slice(s * SEGTOK, (s + 1) * SEGTOK)

            def moments(source, stats, stats_done, result_, result_done_, count):
                for t in range(NT):
                    nc.vector.bn_stats(stats[:, t, :], source[:, t, 0:D]).then_inc(stats_done, 1)
                wait_first(dve, stats_done, NT * count)
                for t in range(NT):
                    nc.vector.bn_aggr(result_[:, t, :], stats[:, t, :]).then_inc(result_done_, 1)

            def slot(b, n, pair):
                if b is not None:
                    nb = number(b)
                    dve.wait_ge(k_done, 2 * (nb + 1))
                    nc.vector.tensor_reduce(k_max[:, :], bank(3, 2).rearrange("p (g c) -> p g c", c=BANK)[0:CH, :, 0:NT * P],
                                            AX.X, ALU.max).then_inc(k_max_done, 1)
                    dve.wait_ge(k_max_done, nb + 1)
                    nc.vector.scalar_tensor_tensor(k_neg[:, :], k_max[:, :], -1.0, bk_col[:, :],
                                                   ALU.mult, ALU.subtract).then_inc(k_neg_done, 1)
                    dve.wait_ge(k_neg_done, nb + 1)
                    nc.vector.tensor_tensor(k_shift[:, :], k_neg[:, :], bk_col[:, :], ALU.add).then_inc(k_shift_done, 1)
                    dve.wait_ge(qv_done, NT * (nb + 1))
                    q_ps = by_head(qv_ps[:, :, 0:D])
                    nc.vector.tensor_reduce(q_max[:, :, :], q_ps, AX.X, ALU.max).then_inc(q_max_done, 1)
                    dve.wait_ge(q_max_done, nb + 1)
                    wait(dve, q_norm_done, nb)
                    nc.vector.tensor_tensor(by_head(q_exp[:, :, :]), q_ps,
                                            q_max[:, :, :].unsqueeze(3).to_broadcast([P, NT, HEADS, HD]),
                                            ALU.subtract).then_inc(q_shifted, 1)
                if n is not None:
                    nn = number(n)
                    dve.wait_ge(s_done, nn + 1)
                    for s in range(2):
                        h = seg_half(s)
                        nc.vector.tensor_reduce(s_max[h, :], s_ps[h, :, h], AX.X, ALU.max).then_inc(s_max_done, 1)
                    nc.vector.tensor_copy(x_tok[n[1]][:, :, D:XD], s_ps[:, :, P:P + NODES]).then_inc(x_router_copied, 1)
                    dve.wait_ge(s_max_done, 2 * (nn + 1))
                    for s in range(2):
                        h = seg_half(s)
                        nc.vector.tensor_tensor(seg_p[h, :, :], s_ps[h, :, h],
                                                s_max[h, :].unsqueeze(2).to_broadcast([SEGTOK, NT, SEGTOK]),
                                                ALU.subtract).then_inc(s_shifted, 1)
                if b is not None:
                    dve.wait_ge(q_exp_done, nb + 1)
                    nc.vector.tensor_reduce(q_sum[:, :, :], by_head(q_exp[:, :, :]), AX.X, ALU.add).then_inc(q_sum_done, 1)
                    dve.wait_ge(q_sum_done, nb + 1)
                    nc.vector.reciprocal(q_rsum[:, :, :], q_sum[:, :, :]).then_inc(q_rsum_done, 1)
                    dve.wait_ge(k_tok_done, nb + 1)
                    nc.vector.tensor_copy(k_tok[:, :, :], k_tok_ps).then_inc(k_tok_copied, 1)
                    nc.vector.reciprocal(k_rsum[:, :], k_sum[:, :]).then_inc(k_rsum_done, 1)
                if n is not None:
                    dve.wait_ge(seg_pt_done, nn + 1)
                    for s in range(2):
                        h = seg_half(s)
                        nc.vector.tensor_copy(seg_pt[h, :, h], seg_pt_ps[:, :, h]).then_inc(seg_pt_copied, 1)
                if b is not None:
                    dve.wait_ge(kv_done, nb + 1)
                    nc.vector.tensor_tensor(kv[:, :, :], kv_ps, head_mask[:, :].unsqueeze(1).to_broadcast([CH, 2, CH]),
                                            ALU.mult).then_inc(kv_masked, 1)
                def finish(i):
                    dve.wait_ge(ffn_done, 2 * pair + i + 1)
                    wait(dve, stored[i], pair * 16)
                    nc.vector.tensor_tensor(result[i][:, :, :], ffn_ps, h2_ext[i][:, :, 0:D], ALU.add).then_inc(result_done, 1)

                if pair is not None:
                    finish(0)
                if n is not None:
                    dve.wait_ge(h_done, nn + 1)
                    nc.vector.reciprocal(seg_rz[:, :], h_ps[:, :, XD]).then_inc(seg_rz_done, 1)
                if b is not None:
                    dve.wait_ge(mix_done, nb + 1)
                    dve.wait_ge(k_rsum_done, nb + 1)
                    for g in range(2):
                        nc.vector.scalar_tensor_tensor(mix[:, g, :], mix_ps[:, g, :], k_rsum[:, g:g + 1], m_const[:, g, :],
                                                       ALU.mult, ALU.add).then_inc(mix_ready, 1)
                if pair is not None:
                    finish(1)
                if n is not None:
                    dve.wait_ge(h_copied, NT * (nn + 1))
                    moments(h_ext[n[1]], stats1, stats1_done, moments1, moments1_done, nn + 1)
                    dve.wait_ge(rstd1_done, nn + 1)
                    wait(dve, y_split_done, 2 * nn)
                    for t in range(NT):
                        nc.vector.tensor_scalar(y[:, t, :], h_ext[n[1]][:, t, 0:D], moments1[:, t, 0:1], rstd1[:, t:t + 1],
                                                ALU.subtract, ALU.mult).then_inc(y_done, 1)
                if b is not None:
                    dve.wait_ge(out_done, nb + 1)
                    wait(dve, logits_done, nb - 1)
                    nc.vector.tensor_tensor(h2_ext[b[1]][:, :, :], out_ps, h_ext[b[1]][:, :, :], ALU.add).then_inc(h2_done, 1)
                    dve.wait_ge(h2_done, nb + 1)
                    moments(h2_ext[b[1]], stats2, stats2_done, moments2, moments2_done, nb + 1)

            schedule(dve, slot)

        @block.tensor
        def _(pe):
            pe.wait_ge(weights_loaded, 16 * SETUP_LOADS)
            pe.wait_ge(const_built, 12)
            for m in range(3):
                for a in range(2):
                    for h in range(2):
                        at = a * D + h * CH
                        last = nc.tensor.transpose(bank(m)[:, at:at + CH], w_nat[:, m, h, a * A0:(a + 1) * A0], ident[0:CH, 0:CH])
            last.then_inc(w_transposed, 1)
            for e in range(2):
                for h in range(2):
                    at = e * D + h * CH
                    last = nc.tensor.transpose(bank(3)[0:CH, at:at + CH], wp_nat[:, h, e * CH:(e + 1) * CH], ident[0:CH, 0:CH])
            last.then_inc(wp_transposed, 1)
            pe.wait_ge(router_ready, 1)
            for g in range(2):
                last = nc.tensor.transpose(bank(4)[0:CH, g * NODES:(g + 1) * NODES], w_in_c[:, g * CH:(g + 1) * CH],
                                           ident[0:NODES, 0:NODES])
            last.then_inc(router_t_done, 1)
            pe.wait_ge(router_ready, 2)
            for e in range(2):
                for h in range(2):
                    last = nc.tensor.matmul(bank(5)[0:CH, e * NODES:(e + 1) * NODES], wp_nat[:, h, e * CH:(e + 1) * CH],
                                            router[:, h, :], start=(h == 0), stop=(h == 1))
            last.then_inc(wp_router_done, 1)
            for h in range(2):
                last = nc.tensor.matmul(bank(6)[0:1, 0:NODES], bp_col[:, h:h + 1], router[:, h, :], start=(h == 0), stop=(h == 1))
            last.then_inc(bp_router_done, 1)
            pe.wait_ge(router_ready, 3)
            for g in range(2):
                o = bank(7)[0:CH, g * XD:(g + 1) * XD]
                nc.tensor.matmul(o, bv_diag[:, g, :], wp_ext[:, g, :], start=True, stop=False)
                last = nc.tensor.matmul(o, head_share[0:1, :], bp_row[0:1, :], start=False, stop=True)
            last.then_inc(m_const_done, 1)
            pe.wait_ge(const_ready, 1)

            HIGH_A, B_CHUNK, LOW_A = range(3)
            passes = [(HIGH_A, w_hi, 0), (HIGH_A, w_lo, 0), (LOW_A, w_hi, 0), (B_CHUNK, w_hi, 1), (B_CHUNK, w_lo, 1)]

            def transposes(out_, tiles, width):
                for t, tile in enumerate(tiles):
                    last_ = nc.tensor.transpose(out_[0:width, t * P:(t + 1) * P], tile, ident[:, :])
                return last_

            def slot(b, n, pair):
                if b is not None:
                    nb = number(b)
                    pe.wait_ge(y_split_done, 2 * (nb + 1))
                    for c in range(3):
                        transposes(yt_ps[c], [y_split[:, t, c * P:(c + 1) * P] for t in range(NT)], P).then_inc(yt_done, 1)
                    wait(pe, h2_done, nb)
                if n is not None:
                    nn = number(n)
                    pe.wait_ge(x_loaded[n[1]], 32 * (n[0] + 1))
                    for c in range(2):
                        transposes(x_ch_ps[c], [x_tok[n[1]][:, t, c * CH:(c + 1) * CH] for t in range(NT)], CH).then_inc(x_ch_done, 1)
                if b is not None:
                    pe.wait_ge(yt_copied, 3 * (nb + 1))
                    for g in range(2):
                        for i, (c, w, a) in enumerate(passes):
                            at = 2 * D + g * CH
                            last_ = nc.tensor.matmul(k_ps[g][0:CH, 0:NT * P], w[:, a, at:at + CH], yt[:, c, :],
                                                     start=(i == 0), stop=(i == len(passes) - 1))
                        last_.then_inc(k_done, 1)
                if n is not None:
                    pe.wait_ge(x_ch_copied, 2 * (nn + 1))
                if b is not None:
                    for t in range(NT):
                        for i, (c, w, a) in enumerate(passes):
                            last_ = nc.tensor.matmul(qv_ps[:, t, 0:2 * D], yt[:, c, t * P:(t + 1) * P], w[:, a, 0:2 * D],
                                                     start=(i == 0), stop=(i == len(passes) - 1))
                            if i == 0:
                                nc.tensor.matmul(qv_ps[:, t, 0:D], ones_r[:, :], bq_split[:, :],
                                                 start=False, stop=False, skip_group_check=True)
                        last_.then_inc(qv_done, 1)
                if n is not None:
                    for t in range(NT):
                        for c in range(2):
                            last_ = nc.tensor.matmul(s_ps[:, t, :], x_ch[:, c, t, 0:P], x_ch[:, c, t, :],
                                                     start=(c == 0), stop=(c == 1))
                    last_.then_inc(s_done, 1)
                if pair is not None:
                    pe.wait_ge(coef_done, pair + 1)
                    if b is None:
                        pe.wait_ge(h2_done, NBATCH)
                    for i in range(2):
                        transposes(coef_ps[i], [coef_split[:, i * NT + t, :] for t in range(NT)], P).then_inc(coef_t_done, 1)
                if b is not None:
                    pe.wait_ge(k_exp_done, 2 * (nb + 1))
                    for t in range(NT):
                        for g in range(2):
                            last_ = nc.tensor.transpose(k_tok_ps[:, t, g * CH:(g + 1) * CH], k_exp[:, g, t * P:(t + 1) * P],
                                                        ident[0:CH, 0:CH])
                    last_.then_inc(k_tok_done, 1)
                if n is not None:
                    if pair is not None:
                        pe.wait_ge(coef_t_copied, 2 * pair + 1)
                    wait_first(pe, seg_exp_done, nn + 1)
                    for t in range(NT):
                        last_ = nc.tensor.transpose(seg_pt_ps[:, t, :], seg_p[:, t, :], ident[:, :])
                    last_.then_inc(seg_pt_done, 1)
                if b is not None:
                    pe.wait_ge(k_tok_copied, nb + 1)
                    pe.wait_ge(v_copied, nb + 1)
                    pe.wait_ge(q_shifted, nb + 1)
                    for g in range(2):
                        h = slice(g * CH, (g + 1) * CH)
                        for t in range(NT):
                            last_ = nc.tensor.matmul(kv_ps[:, g, :], v_tok[:, t, h], k_tok[:, t, h],
                                                     start=(t == 0), stop=(t == NT - 1))
                    last_.then_inc(kv_done, 1)

                def feed_forward(i):
                    pe.wait_ge(coef_t_copied, 2 * pair + i + 1)
                    for t in range(NT):
                        last__ = nc.tensor.matmul(ffn_ps[:, t, :], coef_t[:, i, t * P:(t + 1) * P], w_out_split[:, :],
                                                  start=True, stop=True)
                    last__.then_inc(ffn_done, 1)

                if pair is not None:
                    feed_forward(0)
                if n is not None:
                    pe.wait_ge(seg_pt_copied, 2 * (nn + 1))
                    pe.wait_ge(x_router_copied, nn + 1)
                    if pair is not None:
                        pe.wait_ge(coef_t_copied, 2 * pair + 2)
                    for t in range(NT):
                        last_ = nc.tensor.matmul(h_ps[:, t, :], seg_pt[:, t, :], x_tok[n[1]][:, t, :], start=True, stop=True)
                    last_.then_inc(h_done, 1)
                if b is not None:
                    pe.wait_ge(q_norm_done, nb + 1)
                    for g in range(2):
                        transposes(q_ch_ps[g], [q_norm[:, t, g * CH:(g + 1) * CH] for t in range(NT)], CH).then_inc(q_ch_done, 1)
                    pe.wait_ge(kv_masked, nb + 1)
                    for g in range(2):
                        last_ = nc.tensor.matmul(mix_ps[:, g, :], kv[:, g, :], wp_ext[:, g, :], start=True, stop=True)
                    last_.then_inc(mix_done, 1)
                if pair is not None:
                    pe.wait_ge(result_done, 2 * pair + 1)
                    feed_forward(1)
                if b is not None:
                    pe.wait_ge(q_ch_copied, 2 * (nb + 1))
                    pe.wait_ge(mix_ready, 2 * (nb + 1))
                    if pair is not None:
                        pe.wait_ge(result_done, 2 * pair + 2)
                    for t in range(NT):
                        for g in range(2):
                            last_ = nc.tensor.matmul(out_ps[:, t, :], q_ch[:, g, t * P:(t + 1) * P], mix[:, g, :],
                                                     start=(g == 0), stop=(g == 1))
                    last_.then_inc(out_done, 1)

            schedule(pe, slot)

    return nc


_INS = ["x", "L0_attn_Wq", "L0_attn_bq", "L0_attn_Wk", "L0_attn_bk", "L0_attn_Wv", "L0_attn_bv", "L0_attn_Wp",
        "L0_attn_bp", "L0_ffn_weights_in", "L0_ffn_weights_out"]


def kernel(**inputs):
    import numpy as _np
    import concourse.bacc as _bacc
    from concourse import mybir as _mybir
    from concourse.bass_utils import run_bass_kernel_spmd as _run

    nc = _bacc.Bacc("TRN2", target_bir_lowering=False, num_devices=1)
    arrays, args = {}, []
    for name in _INS:
        a = _np.ascontiguousarray(inputs[name])
        arrays[f"in_{name}_dram"] = a
        args.append(nc.dram_tensor(f"in_{name}_dram", a.shape, _mybir.dt.from_np(a.dtype), kind="ExternalInput").ap())
    batches, rows, width = inputs["x"].shape
    tokens = -(-rows // 128) * 64
    args.append(nc.dram_tensor("out_0_dram", (batches, tokens, width), _mybir.dt.float32, kind="ExternalOutput").ap())
    audio_tower_kernel(nc, *args)
    r = _run(nc, [arrays], core_ids=[0])
    return r.results[0]["out_0_dram"]
```

```python
import concourse.bass as bass
from concourse import mybir
from contextlib import ExitStack


def audio_tower_kernel(nc, x, Wq, bq, Wk, bk, Wv, bv, Wp, bp, W_in, W_out, out):
    F32, F32R = mybir.dt.float32, mybir.dt.float32r
    ALU = mybir.AluOpType
    ACT = mybir.ActivationFunctionType
    AX = mybir.AxisListType

    NBATCH, ROWS, D = x.shape
    SEGMENT, DILATION = 128, 2
    SEGTOK = SEGMENT // DILATION
    NTOK = -(-ROWS // SEGMENT) * SEGTOK
    P = 128
    NT = NTOK // P
    LAST = (ROWS - (NT - 1) * P * DILATION + DILATION - 1) // DILATION
    HD = 16
    HEADS = D // HD
    CH = D // 2
    GH = CH // HD
    NODES = W_in.shape[0]
    XD = D + NODES
    LEAVES = 32
    PAIRS = NBATCH // 2
    BANK = 512
    PAD = 256
    SCALE = float(D) ** -0.5
    EPS = 1e-5
    TREE_STEPS = 11
    A0 = 128
    B0 = D - A0
    SETUP_LOADS = 22
    STEPS_AT_END = 5.0

    ctx = ExitStack()
    with ctx:
        def sb(name, shape, dt=F32):
            return ctx.enter_context(nc.sbuf_tensor(name, shape, dt))

        def sem(name):
            return ctx.enter_context(nc.semaphore(name))

        ident = sb("ident", [P, P])
        head_mask = sb("head_mask", [CH, CH])
        w_nat = sb("w_nat", [CH, 3, 2, 2 * A0])
        w_hi = sb("w_hi", [P, 2, 3 * D], F32R)
        w_lo = sb("w_lo", [P, 2, 3 * D], F32R)
        wp_nat = sb("wp_nat", [CH, 2, D])
        wp_ext = sb("wp_ext", [CH, 2, XD])
        w_in = sb("w_in", [NODES, D])
        w_in_sum = sb("w_in_sum", [NODES, 1])
        w_in_mean = sb("w_in_mean", [NODES, 1])
        w_in_c = sb("w_in_c", [NODES, D])
        router = sb("router", [CH, 2, NODES])
        bq_raw = sb("bq_raw", [64, D])
        bq_round = sb("bq_round", [64, D], F32R)
        bq_split = sb("bq_split", [64, D], F32R)
        ones_r = sb("ones_r", [64, P], F32R)
        bk_col = sb("bk_col", [CH, 2])
        bv_col = sb("bv_col", [CH, 2])
        bp_col = sb("bp_col", [CH, 2])
        bp_row = sb("bp_row", [1, XD])
        head_share = sb("head_share", [1, CH])
        bv_diag = sb("bv_diag", [CH, 2, CH])
        m_const = sb("m_const", [CH, 2, XD])
        w_out_raw = sb("w_out_raw", [P, D])
        w_out_round = sb("w_out_round", [P, D], F32R)
        w_out_split = sb("w_out_split", [P, D], F32R)
        minus_half = sb("minus_half", [P, NT])

        x_tok = [sb(f"x_tok{i}", [P, NT, XD + 1]) for i in range(2)]
        x_ch = sb("x_ch", [CH, 2, NT, P + NODES])
        s_max = sb("s_max", [P, NT])
        seg_p = sb("seg_p", [P, NT, SEGTOK])
        seg_pt = sb("seg_pt", [P, NT, P])
        seg_rz = sb("seg_rz", [P, NT])
        h_ext = [sb(f"h_ext{i}", [P, NT, XD]) for i in range(2)]
        stats1 = sb("stats1", [P, NT, 6])
        moments1 = sb("moments1", [P, NT, 2])
        var1 = sb("var1", [P, NT])
        rstd1 = sb("rstd1", [P, NT])
        y = sb("y", [P, NT, D])
        y_split = sb("y_split", [P, NT, 3 * P])
        yt = sb("yt", [P, 3, NT * P], F32R)
        k_max = sb("k_max", [CH, 2])
        k_neg = sb("k_neg", [CH, 2])
        k_shift = sb("k_shift", [CH, 2])
        k_exp = sb("k_exp", [CH, 2, NT * P])
        k_sum = sb("k_sum", [CH, 2])
        k_rsum = sb("k_rsum", [CH, 2])
        k_tok = sb("k_tok", [P, NT, D])
        v_tok = sb("v_tok", [P, NT, D])
        q_max = sb("q_max", [P, NT, HEADS])
        q_exp = sb("q_exp", [P, NT, D])
        q_sum = sb("q_sum", [P, NT, HEADS])
        q_rsum = sb("q_rsum", [P, NT, HEADS])
        q_norm = sb("q_norm", [P, NT, D])
        q_ch = sb("q_ch", [CH, 2, NT * P])
        kv = sb("kv", [CH, 2, CH])
        mix = sb("mix", [CH, 2, XD])
        h2_ext = sb("h2_ext", [P, 2, NT, XD])
        stats2 = sb("stats2", [P, NT, 6])
        moments2 = sb("moments2", [P, NT, 2])
        var2 = sb("var2", [P, NT])
        rstd2 = sb("rstd2", [P, NT])
        logits = sb("logits", [P, 2, NT, NODES])
        gelu = sb("gelu", [P, 2 * NT, NODES])
        reach = sb("reach", [P, 2 * NT, NODES])
        tail1 = sb("tail1", [P, 2 * NT])
        tail2 = sb("tail2", [P, 2 * NT])
        coef = sb("coef", [P, 2 * NT, LEAVES])
        coef_split = sb("coef_split", [P, 2 * NT, 4 * LEAVES])
        coef_t = sb("coef_t", [P, 2, NT * P], F32R)
        result = sb("result", [P, 2 * NT, D])

        psum = ctx.enter_context(nc.psum_tensor("psum", [P, 8 * BANK], F32))

        def bank(b, n=1):
            return psum[:, b * BANK:(b + n) * BANK]

        def tiles_in(b, width):
            return bank(b, 2).rearrange("p (t c) -> p t c", c=PAD)[:, 0:NT, 0:width]

        yt_ps = [bank(b) for b in (3, 4, 5)]
        x_ch_ps = [bank(6 + c) for c in range(2)]
        k_ps = [bank(3 + c) for c in range(2)]
        qv_ps = bank(5, 3).rearrange("p (t c) -> p t c", c=BANK)
        SW = P + NODES
        s_ps = bank(0)[:, 0:NT * SW].rearrange("p (t c) -> p t c", c=SW)
        coef_ps = [bank(b) for b in (6, 7)]
        k_tok_ps = tiles_in(3, D)
        seg_pt_ps = bank(0)[0:SEGTOK, 0:NT * P].rearrange("p (t c) -> p t c", c=P)
        kv_ps = bank(5)[0:CH, 0:2 * CH].rearrange("p (g c) -> p g c", c=CH)
        ffn_ps = bank(5, 3).rearrange("p (t c) -> p t c", c=PAD)[:, :, 0:D]
        h_ps = tiles_in(1, XD + 1)
        q_ch_ps = [bank(3 + c) for c in range(2)]
        mix_ps = bank(5)[0:CH, 0:2 * XD].rearrange("p (g c) -> p g c", c=XD)
        out_ps = tiles_in(1, XD)

        const_built, tiles_cleared = sem("const_built"), sem("tiles_cleared")
        weights_loaded, w_transposed, wp_transposed = sem("weights_loaded"), sem("w_transposed"), sem("wp_transposed")
        setup_dve, router_ready = sem("setup_dve"), sem("router_ready")
        router_t_done, wp_router_done, bp_router_done = sem("router_t_done"), sem("wp_router_done"), sem("bp_router_done")
        m_const_done, const_ready = sem("m_const_done"), sem("const_ready")
        x_loaded = [sem("x_loaded0"), sem("x_loaded1")]
        x_ch_done, x_ch_copied = sem("x_ch_done"), sem("x_ch_copied")
        s_done, s_max_done, x_router_copied, s_shifted = sem("s_done"), sem("s_max_done"), sem("x_router_copied"), sem("s_shifted")
        seg_exp_done, seg_pt_done, seg_pt_copied = sem("seg_exp_done"), sem("seg_pt_done"), sem("seg_pt_copied")
        h_done, seg_rz_done, h_copied = sem("h_done"), sem("seg_rz_done"), sem("h_copied")
        stats1_done, moments1_done, var1_done, rstd1_done = sem("stats1_done"), sem("moments1_done"), sem("var1_done"), sem("rstd1_done")
        y_done, y_high_done, y_split_done = sem("y_done"), sem("y_high_done"), sem("y_split_done")
        yt_done, yt_copied = sem("yt_done"), sem("yt_copied")
        k_done, k_max_done, k_neg_done, k_shift_done = sem("k_done"), sem("k_max_done"), sem("k_neg_done"), sem("k_shift_done")
        k_exp_done, k_tok_done, k_tok_copied, k_rsum_done = sem("k_exp_done"), sem("k_tok_done"), sem("k_tok_copied"), sem("k_rsum_done")
        qv_done, v_copied = sem("qv_done"), sem("v_copied")
        q_max_done, q_shifted, q_exp_done, q_sum_done, q_rsum_done, q_norm_done = (
            sem("q_max_done"), sem("q_shifted"), sem("q_exp_done"), sem("q_sum_done"), sem("q_rsum_done"), sem("q_norm_done"))
        q_ch_done, q_ch_copied = sem("q_ch_done"), sem("q_ch_copied")
        kv_done, kv_masked, mix_done, mix_ready = sem("kv_done"), sem("kv_masked"), sem("mix_done"), sem("mix_ready")
        out_done, h2_done = sem("out_done"), sem("h2_done")
        stats2_done, moments2_done, var2_done, rstd2_done, logits_done = (
            sem("stats2_done"), sem("moments2_done"), sem("var2_done"), sem("rstd2_done"), sem("logits_done"))
        gelu_done, coef_high_done, coef_done = sem("gelu_done"), sem("coef_high_done"), sem("coef_done")
        tree_step = sem("tree_step")
        coef_t_done, coef_t_copied, ffn_done, result_done = sem("coef_t_done"), sem("coef_t_copied"), sem("ffn_done"), sem("result_done")
        wait_passed = sem("wait_passed")
        stored = sem("stored")

        def wait(eng, semaphore, count):
            if not (isinstance(count, int) and count <= 0):
                eng.wait_ge(semaphore, count)

        def wait_first(eng, semaphore, count):
            eng.wait_ge(semaphore, count)
            eng.nop().then_inc(wait_passed, 1)

        def schedule(eng, slot, looped=PAIRS - 1):
            slot(None, None, (0, 0), None)
            slot(None, (0, 0), (0, 1), None)
            slot((0, 0), (0, 1), (1, 0), None)
            slot((0, 1), (1, 0), (1, 1), None)
            with eng.Fori(1, looped) as j:
                slot((j, 0), (j, 1), (j + 1, 0), j - 1)
                slot((j, 1), (j + 1, 0), (j + 1, 1), None)
            for j in range(looped, PAIRS - 1):
                slot((j, 0), (j, 1), (j + 1, 0), j - 1)
                slot((j, 1), (j + 1, 0), (j + 1, 1), None)
            last = PAIRS - 1
            slot((last, 0), (last, 1), None, last - 1)
            slot((last, 1), None, None, None)
            slot(None, None, None, last)

        def number(batch):
            return 2 * batch[0] + batch[1]

        coef4 = coef_split[:, :, :].bitcast(F32R).rearrange("p t (s e l) -> p t s e l", e=2, l=LEAVES)
        coef4_f = coef_split[:, :, :].rearrange("p t (s e l) -> p t s e l", e=2, l=LEAVES)
        coef_twice = coef[:, :, :].unsqueeze(2).to_broadcast([P, 2 * NT, 2, LEAVES])

        block = ctx.enter_context(nc.Block())

        @block.sync
        def _(sp):
            for m, w in enumerate((Wq, Wv, Wk)):
                rows = w.rearrange("(h o) i -> o h i", h=2)
                sp.dma_start(w_nat[:, m, :, 0:D], rows).then_inc(weights_loaded, 16)
                sp.dma_start(w_nat[:, m, :, D:2 * A0], rows[:, :, A0:D]).then_inc(weights_loaded, 16)
            sp.dma_start(wp_nat[:, :, :], Wp.rearrange("(h o) i -> o h i", h=2)).then_inc(weights_loaded, 16)
            sp.dma_start(w_in[:, :], W_in).then_inc(weights_loaded, 16)
            for col, b in ((bk_col, bk), (bv_col, bv), (bp_col, bp)):
                sp.dma_start(col[:, :], b.rearrange("(g c) -> c g", g=2),
                             allow_slow_non_contiguous=True).then_inc(weights_loaded, 16)
            sp.dma_start(bp_row[0:1, 0:D], bp.rearrange("(a c) -> a c", a=1)).then_inc(weights_loaded, 16)
            sp.wait_ge(tiles_cleared, 4)
            for part in (0, 32):
                sp.dma_start(bq_raw[part:part + 1, :], bq.rearrange("(a c) -> a c", a=1)).then_inc(weights_loaded, 16)
            first = NODES // 2
            for s in range(4):
                at = s * LEAVES
                sp.dma_start(w_out_raw[at:at + NODES - 1, :], W_out[1:NODES, :]).then_inc(weights_loaded, 16)
                sp.dma_start(w_out_raw[at + NODES - 1:at + NODES - 1 + NODES - first, :],
                             W_out[NODES - 1:NODES, :].to_broadcast([NODES - first, D])).then_inc(weights_loaded, 16)

            def load_x(batch):
                j, p = batch
                rows = x[bass.ds(number(batch), 1), :, :].rearrange("a r c -> (a r) c")
                whole = rows[0:(NT - 1) * P * DILATION, :].rearrange("(t q s) c -> q t s c", q=P, s=DILATION)
                sp.dma_start(x_tok[p][:, 0:NT - 1, 0:D], whole[:, :, 0, :]).then_inc(x_loaded[p], 16)
                rest = rows[(NT - 1) * P * DILATION:ROWS, :].rearrange("(q s) c -> q s c", s=DILATION)
                sp.dma_start(x_tok[p][0:LAST, NT - 1, 0:D], rest[:, 0, :]).then_inc(x_loaded[p], 16)

            load_x((0, 0))
            load_x((0, 1))

            def store(pair):
                sp.wait_ge(result_done, pair + 1)
                dst = out[bass.ds(2 * pair, 2), :, :].rearrange("a (t q) c -> q (a t) c", q=P)
                sp.dma_start(dst, result[:, :, :]).then_inc(stored, 16)

            def slot(b, n, m, pair):
                if n is not None and not (isinstance(n[0], int) and n[0] + 1 >= PAIRS):
                    sp.wait_ge(h_done, number(n) + 1)
                    load_x((n[0] + 1, n[1]))
                if pair is not None:
                    store(pair)

            schedule(sp, slot, looped=PAIRS - 2)
            sp.wait_ge(stored, 16 * PAIRS)

        @block.gpsimd
        def _(pool):
            nc.gpsimd.memset(x_tok[0][:, :, :], 0.0).then_inc(tiles_cleared, 1)
            nc.gpsimd.memset(x_tok[1][:, :, :], 0.0).then_inc(tiles_cleared, 1)
            nc.gpsimd.memset(bq_raw[:, :], 0.0).then_inc(tiles_cleared, 1)
            nc.gpsimd.memset(w_out_raw[:, :], 0.0).then_inc(tiles_cleared, 1)
            nc.gpsimd.memset(ident[:, :], 0.0).then_inc(const_built, 1)
            nc.gpsimd.memset(head_mask[:, :], float(HD) ** -0.5).then_inc(const_built, 1)
            pool.wait_ge(const_built, 2)
            nc.gpsimd.affine_select(out=ident[:, :], in_=ident[:, :], compare_op=ALU.not_equal, fill=1.0,
                                    base=0, pattern=[[-1, P]], channel_multiplier=1).then_inc(const_built, 1)
            heads = head_mask[:, :].rearrange("p (g c) -> p g c", c=HD)
            nc.gpsimd.affine_select(out=heads, in_=heads, compare_op=ALU.is_ge, fill=0.0, base=0,
                                    pattern=[[-HD, GH], [0, HD]], channel_multiplier=1).then_inc(const_built, 1)
            pool.wait_ge(const_built, 4)
            nc.gpsimd.affine_select(out=heads, in_=heads, compare_op=ALU.is_ge, fill=0.0, base=HD - 1,
                                    pattern=[[HD, GH], [0, HD]], channel_multiplier=-1).then_inc(const_built, 1)
            nc.gpsimd.memset(ones_r[:, :].bitcast(F32), 1.0).then_inc(const_built, 1)
            nc.gpsimd.memset(head_share[:, :], 1.0 / HEADS).then_inc(const_built, 1)
            nc.gpsimd.memset(minus_half[:, :], -0.5).then_inc(const_built, 1)
            nc.gpsimd.memset(coef[:, :, :], 0.0).then_inc(const_built, 1)
            nc.gpsimd.memset(seg_pt[:, :, :], 0.0).then_inc(const_built, 1)
            pool.wait_ge(const_built, 10)
            pool.wait_ge(x_loaded[0], 32)
            for i in range(2):
                nc.gpsimd.memset(x_tok[i][:, :, XD:XD + 1], 1.0).then_inc(const_built, 1)

            HALF = NODES // 2
            flat_logits = logits[:, :, :, :].rearrange("p b t n -> p (b t) n")

            def step(pair, k, instruction):
                instruction.then_inc(tree_step, 1)
                wait_first(pool, tree_step, TREE_STEPS * pair + k if isinstance(pair, int) else pair * TREE_STEPS + k)

            def twice(a):
                return a.unsqueeze(3).to_broadcast([P, 2 * NT, a.shape[2], 2])

            child = reach[:, :, 1:NODES].rearrange("p t (n c) -> p t n c", c=2)

            def tree_paths(pair):
                wait_first(pool, logits_done, 2 * pair + 2)
                nc.gpsimd.tensor_scalar(child[:, :, :, 1], flat_logits[:, :, 0:HALF], 0.0, None, ALU.is_gt)
                step(pair, 1, nc.gpsimd.tensor_scalar(child[:, :, :, 0], flat_logits[:, :, 0:HALF], 0.0, None, ALU.is_le))
                for k, (lo, hi) in enumerate(((3, 7), (7, 15), (15, NODES))):
                    kids = reach[:, :, lo:hi].rearrange("p t (n c) -> p t n c", c=2)
                    step(pair, 2 + k, nc.gpsimd.tensor_tensor(kids, kids, twice(reach[:, :, (lo - 1) // 2:(hi - 1) // 2]), ALU.mult))
                step(pair, 5, nc.gpsimd.tensor_tensor(tail1[:, :], reach[:, :, HALF], reach[:, :, 5], ALU.add))
                step(pair, 6, nc.gpsimd.tensor_tensor(tail2[:, :], tail1[:, :], reach[:, :, 6], ALU.add))

            def tree_coefficients(pair):
                pool.wait_ge(gelu_done, pair + 1)
                head = coef[:, :, 0:NODES - 1].rearrange("p t (n c) -> p t n c", c=2)
                step(pair, 7, nc.gpsimd.tensor_tensor(head, child, twice(gelu[:, :, 0:HALF]), ALU.mult))
                step(pair, 8, nc.gpsimd.tensor_tensor(reach[:, :, NODES - 1], reach[:, :, NODES - 1], tail2[:, :], ALU.add))
                step(pair, 9, nc.gpsimd.tensor_tensor(coef[:, :, NODES - 1:NODES - 1 + NODES - HALF], reach[:, :, HALF:NODES],
                                                      gelu[:, :, HALF:NODES], ALU.mult))
                step(pair, 10, nc.gpsimd.tensor_scalar(tail1[:, :], gelu[:, :, NODES - 1], STEPS_AT_END, None, ALU.mult))
                step(pair, 11, nc.gpsimd.tensor_tensor(coef[:, :, LEAVES - 2], coef[:, :, LEAVES - 2], tail1[:, :], ALU.add))

            def split_coefficients(pair):
                pool.wait_ge(coef_high_done, pair + 1)
                nc.gpsimd.tensor_tensor(coef4[:, :, :, 1, :], coef_twice, coef4_f[:, :, :, 0, :],
                                        ALU.subtract).then_inc(coef_done, 1)

            def slot(b, n, m, pair):
                if pair is not None:
                    tree_paths(pair)
                if pair is not None:
                    tree_coefficients(pair)
                if n is not None:
                    wait_first(pool, moments1_done, NT * (number(n) + 1))
                    nc.gpsimd.tensor_scalar(var1[:, :], moments1[:, :, 1], EPS, None, ALU.add).then_inc(var1_done, 1)
                    pool.wait_ge(var1_done, number(n) + 1)
                    nc.gpsimd.tensor_tensor(rstd1[:, :], var1[:, :], minus_half[:, :], ALU.pow).then_inc(rstd1_done, 1)
                if pair is not None:
                    split_coefficients(pair)
                if b is not None:
                    pool.wait_ge(q_rsum_done, number(b) + 1)
                    wait(pool, q_ch_done, 2 * number(b))
                    by_head = q_norm[:, :, :].rearrange("p t (h c) -> p t h c", c=HD)
                    nc.gpsimd.tensor_tensor(by_head, q_exp[:, :, :].rearrange("p t (h c) -> p t h c", c=HD),
                                            q_rsum[:, :, :].unsqueeze(3).to_broadcast([P, NT, HEADS, HD]),
                                            ALU.mult).then_inc(q_norm_done, 1)
                if n is not None:
                    pool.wait_ge(y_high_done, number(n) + 1)
                    high = y_split[:, :, 0:D]
                    nc.gpsimd.tensor_tensor(y_split[:, :, D:2 * A0].bitcast(F32R), y[:, :, A0:D],
                                            high[:, :, A0:D], ALU.subtract).then_inc(y_split_done, 1)
                    nc.gpsimd.tensor_tensor(y_split[:, :, 2 * A0:3 * P].bitcast(F32R), y[:, :, 0:A0],
                                            high[:, :, 0:A0], ALU.subtract).then_inc(y_split_done, 1)
                if b is not None:
                    wait_first(pool, moments2_done, NT * (number(b) + 1))
                    nc.gpsimd.tensor_scalar(var2[:, :], moments2[:, :, 1], EPS, None, ALU.add).then_inc(var2_done, 1)
                    pool.wait_ge(var2_done, number(b) + 1)
                    nc.gpsimd.tensor_tensor(rstd2[:, :], var2[:, :], minus_half[:, :], ALU.pow).then_inc(rstd2_done, 1)
                    pool.wait_ge(rstd2_done, number(b) + 1)
                    wait(pool, gelu_done, b[0])
                    nc.gpsimd.tensor_tensor(logits[:, b[1], :, :], h2_ext[:, b[1], :, D:XD],
                                            rstd2[:, :].unsqueeze(2).to_broadcast([P, NT, NODES]),
                                            ALU.mult).then_inc(logits_done, 1)

            schedule(pool, slot)

        @block.scalar
        def _(act):
            def slot(b, n, m, pair):
                if b is not None:
                    for c in range(3):
                        act.wait_ge(yt_done, 3 * number(b) + c + 1)
                        nc.scalar.activation(yt[:, c, :], yt_ps[c][:, 0:NT * P], ACT.Copy).then_inc(yt_copied, 1)
                if m is not None:
                    for c in range(2):
                        act.wait_ge(x_ch_done, 2 * number(m) + c + 1)
                        nc.scalar.activation(x_ch[:, c, :, 0:P],
                                             x_ch_ps[c][0:CH, 0:NT * P].rearrange("p (t c) -> p t c", c=P),
                                             ACT.Copy).then_inc(x_ch_copied, 1)
                if n is not None:
                    act.wait_ge(seg_rz_done, number(n) + 1)
                    for t in range(NT):
                        nc.scalar.activation(h_ext[n[1]][:, t, :], h_ps[:, t, 0:XD], ACT.Copy,
                                             scale=seg_rz[:, t:t + 1]).then_inc(h_copied, 1)
                if pair is not None:
                    act.wait_ge(logits_done, 2 * pair + 2)
                    wait(act, coef_done, pair)
                    nc.scalar.activation(gelu[:, :, :], logits[:, :, :, :].rearrange("p b t n -> p (b t) n"),
                                         ACT.Gelu).then_inc(gelu_done, 1)
                if b is not None:
                    act.wait_ge(k_shift_done, number(b) + 1)
                    for g in range(2):
                        nc.scalar.activation(k_exp[:, g, :], k_ps[g][0:CH, 0:NT * P], ACT.Exp,
                                             bias=k_shift[:, g:g + 1],
                                             accum_out=k_sum[:, g:g + 1]).then_inc(k_exp_done, 1)
                if b is not None:
                    act.wait_ge(q_shifted, NT * number(b) + 1)
                    nc.scalar.activation(v_tok[:, 0, :], qv_ps[:, 0, D:2 * D], ACT.Copy).then_inc(v_copied, 1)
                    act.wait_ge(k_tok_done, number(b) + 1)
                    nc.scalar.activation(k_tok[:, :, :], k_tok_ps, ACT.Copy).then_inc(k_tok_copied, 1)
                    act.wait_ge(q_shifted, NT * (number(b) + 1))
                    nc.scalar.activation(v_tok[:, 1:NT, :], qv_ps[:, 1:NT, D:2 * D], ACT.Copy).then_inc(v_copied, 1)
                    nc.scalar.activation(q_exp[:, :, :], q_exp[:, :, :], ACT.Exp).then_inc(q_exp_done, 1)
                if pair is not None:
                    act.wait_ge(tree_step, TREE_STEPS * (pair + 1))
                    nc.scalar.activation(coef4[:, :, :, 0, :], coef_twice, ACT.Copy).then_inc(coef_high_done, 1)
                if n is not None:
                    wait(act, yt_done, 3 * number(n))
                    act.wait_ge(y_done, NT * (number(n) + 1))
                    nc.scalar.activation(y_split[:, :, 0:D].bitcast(F32R), y[:, :, :], ACT.Copy).then_inc(y_high_done, 1)
                if b is not None:
                    for g in range(2):
                        act.wait_ge(q_ch_done, 2 * number(b) + g + 1)
                        nc.scalar.activation(q_ch[:, g, :], q_ch_ps[g][0:CH, 0:NT * P], ACT.Copy).then_inc(q_ch_copied, 1)
                if pair is not None:
                    for i in range(2):
                        act.wait_ge(coef_t_done, 2 * pair + i + 1)
                        nc.scalar.activation(coef_t[:, i, :], coef_ps[i][:, 0:NT * P], ACT.Copy).then_inc(coef_t_copied, 1)
                if m is not None:
                    act.wait_ge(s_shifted, 2 * (number(m) + 1))
                    nc.scalar.activation(seg_p[:, :, :], seg_p[:, :, :], ACT.Exp, scale=SCALE).then_inc(seg_exp_done, 1)

            schedule(act, slot)

        @block.vector
        def _(dve):
            steps = [0]

            def step(instruction):
                steps[0] += 1
                instruction.then_inc(setup_dve, 1)
                dve.wait_ge(setup_dve, steps[0])

            dve.wait_ge(weights_loaded, 16 * SETUP_LOADS)
            step(nc.vector.tensor_reduce(w_in_sum[:, :], w_in[:, :], AX.X, ALU.add))
            step(nc.vector.tensor_scalar(w_in_mean[:, :], w_in_sum[:, :], 1.0 / D, None, ALU.mult))
            nc.vector.tensor_scalar(w_in_c[:, :], w_in[:, :], w_in_mean[:, 0:1], None, ALU.subtract).then_inc(router_ready, 1)
            w_ps = bank(0, 3).rearrange("p (m c) -> p m c", c=BANK)[:, :, 0:2 * D].rearrange("p m (a o) -> p a m o", a=2)
            dve.wait_ge(w_transposed, 1)
            for a in range(2):
                nc_hi = w_hi[:, a, :].rearrange("p (m o) -> p m o", m=3)
                step(nc.vector.tensor_copy(nc_hi, w_ps[:, a]))
                step(nc.vector.tensor_tensor(w_lo[:, a, :].rearrange("p (m o) -> p m o", m=3), w_ps[:, a],
                                             nc_hi.bitcast(F32), ALU.subtract))
            dve.wait_ge(wp_transposed, 1)
            step(nc.vector.tensor_copy(wp_ext[:, :, 0:D], bank(3)[0:CH, 0:2 * D].rearrange("p (g c) -> p g c", g=2)))
            step(nc.vector.tensor_copy(bq_round[:, :], bq_raw[:, :]))
            step(nc.vector.tensor_copy(bq_split[0:32, :], bq_round[0:32, :].bitcast(F32)))
            step(nc.vector.tensor_tensor(bq_split[32:64, :], bq_raw[32:64, :], bq_round[32:64, :].bitcast(F32), ALU.subtract))
            step(nc.vector.tensor_copy(w_out_round[:, :], w_out_raw[:, :]))
            step(nc.vector.tensor_copy(w_out_split[0:64, :], w_out_round[0:64, :].bitcast(F32)))
            step(nc.vector.tensor_tensor(w_out_split[64:P, :], w_out_raw[64:P, :], w_out_round[64:P, :].bitcast(F32), ALU.subtract))
            dve.wait_ge(router_t_done, 1)
            router_ps = bank(4)[0:CH, 0:2 * NODES].rearrange("p (g n) -> p g n", g=2)
            nc.vector.tensor_copy(router[:, :, :], router_ps).then_inc(router_ready, 1)
            step(nc.vector.tensor_copy(x_ch[:, :, :, P:P + NODES],
                                       router_ps.unsqueeze(2).to_broadcast([CH, 2, NT, NODES])))
            dve.wait_ge(wp_router_done, 1)
            step(nc.vector.tensor_copy(wp_ext[:, :, D:XD], bank(5)[0:CH, 0:2 * NODES].rearrange("p (g n) -> p g n", g=2)))
            dve.wait_ge(bp_router_done, 1)
            step(nc.vector.tensor_copy(bp_row[0:1, D:XD], bank(6)[0:1, 0:NODES]))
            for g in range(2):
                step(nc.vector.tensor_scalar(bv_diag[:, g, :], head_mask[:, :], bv_col[:, g:g + 1], None, ALU.mult))
            nc.vector.tensor_copy(k_sum[:, :], bk_col[:, :]).then_inc(router_ready, 1)
            dve.wait_ge(m_const_done, 1)
            step(nc.vector.tensor_copy(m_const[:, :, :], bank(7)[0:CH, 0:2 * XD].rearrange("p (g c) -> p g c", g=2)))
            nc.vector.nop().then_inc(const_ready, 1)

            def by_head(a):
                return a.rearrange("p t (h c) -> p t h c", c=HD)

            def seg_half(s):
                return slice(s * SEGTOK, (s + 1) * SEGTOK)

            def moments(source, stats, stats_done, result_, result_done_, count):
                for t in range(NT):
                    nc.vector.bn_stats(stats[:, t, :], source[:, t, 0:D]).then_inc(stats_done, 1)
                wait_first(dve, stats_done, NT * count)
                for t in range(NT):
                    nc.vector.bn_aggr(result_[:, t, :], stats[:, t, :]).then_inc(result_done_, 1)

            def slot(b, n, m, pair):
                nb = None if b is None else number(b)
                nn = None if n is None else number(n)
                nm = None if m is None else number(m)

                def shift_queries(t):
                    dve.wait_ge(qv_done, NT * nb + t + 1)
                    q_ps = qv_ps[:, t, 0:D].rearrange("p (h c) -> p h c", c=HD)
                    nc.vector.tensor_reduce(q_max[:, t, :], q_ps, AX.X, ALU.max).then_inc(q_max_done, 1)
                    dve.wait_ge(q_max_done, NT * nb + t + 1)
                    nc.vector.tensor_tensor(q_exp[:, t, :].rearrange("p (h c) -> p h c", c=HD), q_ps,
                                            q_max[:, t, :].unsqueeze(2).to_broadcast([P, HEADS, HD]),
                                            ALU.subtract).then_inc(q_shifted, 1)

                if n is not None:
                    dve.wait_ge(h_done, nn + 1)
                    nc.vector.reciprocal(seg_rz[:, :], h_ps[:, :, XD]).then_inc(seg_rz_done, 1)
                if b is not None:
                    for g in range(2):
                        dve.wait_ge(k_done, 2 * nb + g + 1)
                        nc.vector.tensor_reduce(k_max[:, g:g + 1], k_ps[g][0:CH, 0:NT * P], AX.X, ALU.max).then_inc(k_max_done, 1)
                    dve.wait_ge(k_max_done, 2 * (nb + 1))
                    nc.vector.scalar_tensor_tensor(k_neg[:, :], k_max[:, :], -1.0, bk_col[:, :],
                                                   ALU.mult, ALU.subtract).then_inc(k_neg_done, 1)
                    dve.wait_ge(k_neg_done, nb + 1)
                    nc.vector.tensor_tensor(k_shift[:, :], k_neg[:, :], bk_col[:, :], ALU.add).then_inc(k_shift_done, 1)
                    wait(dve, q_norm_done, nb)
                    for t in range(NT):
                        shift_queries(t)
                if n is not None:
                    dve.wait_ge(h_copied, NT * (nn + 1))
                    moments(h_ext[n[1]], stats1, stats1_done, moments1, moments1_done, nn + 1)
                if b is not None:
                    dve.wait_ge(q_exp_done, nb + 1)
                    nc.vector.tensor_reduce(q_sum[:, :, :], by_head(q_exp[:, :, :]), AX.X, ALU.add).then_inc(q_sum_done, 1)
                    nc.vector.reciprocal(k_rsum[:, :], k_sum[:, :]).then_inc(k_rsum_done, 1)
                    dve.wait_ge(q_sum_done, nb + 1)
                    nc.vector.reciprocal(q_rsum[:, :, :], q_sum[:, :, :]).then_inc(q_rsum_done, 1)
                    dve.wait_ge(kv_done, nb + 1)
                    nc.vector.tensor_tensor(kv[:, :, :], kv_ps, head_mask[:, :].unsqueeze(1).to_broadcast([CH, 2, CH]),
                                            ALU.mult).then_inc(kv_masked, 1)
                if n is not None:
                    dve.wait_ge(rstd1_done, nn + 1)
                    wait(dve, y_split_done, 2 * nn)
                    for t in range(NT):
                        nc.vector.tensor_scalar(y[:, t, :], h_ext[n[1]][:, t, 0:D], moments1[:, t, 0:1], rstd1[:, t:t + 1],
                                                ALU.subtract, ALU.mult).then_inc(y_done, 1)
                if b is not None:
                    dve.wait_ge(mix_done, nb + 1)
                    dve.wait_ge(k_rsum_done, nb + 1)
                    for g in range(2):
                        nc.vector.scalar_tensor_tensor(mix[:, g, :], mix_ps[:, g, :], k_rsum[:, g:g + 1], m_const[:, g, :],
                                                       ALU.mult, ALU.add).then_inc(mix_ready, 1)
                if m is not None:
                    dve.wait_ge(s_done, NT * (nm + 1))
                    for s in range(2):
                        h = seg_half(s)
                        nc.vector.tensor_reduce(s_max[h, :], s_ps[h, :, h], AX.X, ALU.max).then_inc(s_max_done, 1)
                    nc.vector.tensor_copy(x_tok[m[1]][:, :, D:XD], s_ps[:, :, P:P + NODES]).then_inc(x_router_copied, 1)
                    dve.wait_ge(s_max_done, 2 * (nm + 1))
                    for s in range(2):
                        h = seg_half(s)
                        nc.vector.tensor_tensor(seg_p[h, :, :], s_ps[h, :, h],
                                                s_max[h, :].unsqueeze(2).to_broadcast([SEGTOK, NT, SEGTOK]),
                                                ALU.subtract).then_inc(s_shifted, 1)
                if m is not None:
                    dve.wait_ge(seg_pt_done, nm + 1)
                    dve.wait_ge(x_router_copied, nm + 1)
                    for s in range(2):
                        h = seg_half(s)
                        nc.vector.tensor_copy(seg_pt[h, :, h], seg_pt_ps[:, :, h]).then_inc(seg_pt_copied, 1)
                if pair is not None:
                    dve.wait_ge(ffn_done, pair + 1)
                    wait(dve, stored, pair * 16)
                    nc.vector.tensor_tensor(result[:, :, :], ffn_ps, h2_ext[:, :, :, 0:D].rearrange("p b t c -> p (b t) c"),
                                            ALU.add).then_inc(result_done, 1)
                if b is not None:
                    dve.wait_ge(out_done, NT * (nb + 1))
                    wait(dve, logits_done, nb - 1)
                    wait(dve, result_done, b[0])
                    nc.vector.tensor_tensor(h2_ext[:, b[1], :, :], out_ps, h_ext[b[1]][:, :, :], ALU.add).then_inc(h2_done, 1)
                    dve.wait_ge(h2_done, nb + 1)
                    moments(h2_ext[:, b[1]], stats2, stats2_done, moments2, moments2_done, nb + 1)

            schedule(dve, slot)

        @block.tensor
        def _(pe):
            pe.wait_ge(weights_loaded, 16 * SETUP_LOADS)
            pe.wait_ge(const_built, 12)
            for m in range(3):
                for a in range(2):
                    for h in range(2):
                        at = a * D + h * CH
                        last = nc.tensor.transpose(bank(m)[:, at:at + CH], w_nat[:, m, h, a * A0:(a + 1) * A0], ident[0:CH, 0:CH])
            last.then_inc(w_transposed, 1)
            for e in range(2):
                for h in range(2):
                    at = e * D + h * CH
                    last = nc.tensor.transpose(bank(3)[0:CH, at:at + CH], wp_nat[:, h, e * CH:(e + 1) * CH], ident[0:CH, 0:CH])
            last.then_inc(wp_transposed, 1)
            pe.wait_ge(router_ready, 1)
            for g in range(2):
                last = nc.tensor.transpose(bank(4)[0:CH, g * NODES:(g + 1) * NODES], w_in_c[:, g * CH:(g + 1) * CH],
                                           ident[0:NODES, 0:NODES])
            last.then_inc(router_t_done, 1)
            pe.wait_ge(router_ready, 2)
            for e in range(2):
                for h in range(2):
                    last = nc.tensor.matmul(bank(5)[0:CH, e * NODES:(e + 1) * NODES], wp_nat[:, h, e * CH:(e + 1) * CH],
                                            router[:, h, :], start=(h == 0), stop=(h == 1))
            last.then_inc(wp_router_done, 1)
            for h in range(2):
                last = nc.tensor.matmul(bank(6)[0:1, 0:NODES], bp_col[:, h:h + 1], router[:, h, :], start=(h == 0), stop=(h == 1))
            last.then_inc(bp_router_done, 1)
            pe.wait_ge(router_ready, 3)
            for g in range(2):
                o = bank(7)[0:CH, g * XD:(g + 1) * XD]
                nc.tensor.matmul(o, bv_diag[:, g, :], wp_ext[:, g, :], start=True, stop=False)
                last = nc.tensor.matmul(o, head_share[0:1, :], bp_row[0:1, :], start=False, stop=True)
            last.then_inc(m_const_done, 1)
            pe.wait_ge(const_ready, 1)

            HIGH_A, B_CHUNK, LOW_A = range(3)
            passes = [(HIGH_A, w_hi, 0), (HIGH_A, w_lo, 0), (LOW_A, w_hi, 0), (B_CHUNK, w_hi, 1), (B_CHUNK, w_lo, 1)]

            def transposes(out_, tiles, width):
                for t, tile in enumerate(tiles):
                    last_ = nc.tensor.transpose(out_[0:width, t * P:(t + 1) * P], tile, ident[:, :])
                return last_

            def slot(b, n, m, pair):
                nb = None if b is None else number(b)
                nn = None if n is None else number(n)
                nm = None if m is None else number(m)

                def keys(g):
                    for i, (c, w, a) in enumerate(passes):
                        at = 2 * D + g * CH
                        last_ = nc.tensor.matmul(k_ps[g][0:CH, 0:NT * P], w[:, a, at:at + CH], yt[:, c, :],
                                                 start=(i == 0), stop=(i == len(passes) - 1))
                    last_.then_inc(k_done, 1)

                def queries_and_values(t):
                    for i, (c, w, a) in enumerate(passes):
                        last_ = nc.tensor.matmul(qv_ps[:, t, 0:2 * D], yt[:, c, t * P:(t + 1) * P], w[:, a, 0:2 * D],
                                                 start=(i == 0), stop=(i == len(passes) - 1))
                        if i == 0:
                            nc.tensor.matmul(qv_ps[:, t, 0:D], ones_r[:, :], bq_split[:, :],
                                             start=False, stop=False, skip_group_check=True)
                    last_.then_inc(qv_done, 1)

                def scores(t):
                    for c in range(2):
                        last_ = nc.tensor.matmul(s_ps[:, t, :], x_ch[:, c, t, 0:P], x_ch[:, c, t, :],
                                                 start=(c == 0), stop=(c == 1))
                    last_.then_inc(s_done, 1)

                def query_transposes(g):
                    transposes(q_ch_ps[g], [q_norm[:, t, g * CH:(g + 1) * CH] for t in range(NT)], CH).then_inc(q_ch_done, 1)

                def mixed(t):
                    for g in range(2):
                        last_ = nc.tensor.matmul(out_ps[:, t, :], q_ch[:, g, t * P:(t + 1) * P], mix[:, g, :],
                                                 start=(g == 0), stop=(g == 1))
                    last_.then_inc(out_done, 1)

                if b is not None:
                    pe.wait_ge(y_split_done, 2 * (nb + 1))
                    for c in range(3):
                        if c == 2 and b[1] == 1:
                            wait(pe, result_done, b[0])
                        transposes(yt_ps[c], [y_split[:, t, c * P:(c + 1) * P] for t in range(NT)], P).then_inc(yt_done, 1)
                if m is not None:
                    pe.wait_ge(x_loaded[m[1]], 32 * (m[0] + 1))
                    for c in range(2):
                        transposes(x_ch_ps[c], [x_tok[m[1]][:, t, c * CH:(c + 1) * CH] for t in range(NT)], CH).then_inc(x_ch_done, 1)
                if n is not None:
                    pe.wait_ge(seg_pt_copied, 2 * (nn + 1))
                    wait(pe, h2_done, nn - 1)
                    for t in range(NT):
                        last_ = nc.tensor.matmul(h_ps[:, t, :], seg_pt[:, t, :], x_tok[n[1]][:, t, :], start=True, stop=True)
                    last_.then_inc(h_done, 1)
                if b is not None:
                    pe.wait_ge(yt_copied, 3 * (nb + 1))
                    keys(0)
                    keys(1)
                    if m is not None:
                        pe.wait_ge(x_ch_copied, 2 * (nm + 1))
                    for t in range(NT):
                        queries_and_values(t)
                if m is not None:
                    pe.wait_ge(x_ch_copied, 2 * (nm + 1))
                    if pair is not None:
                        scores(0)
                if b is not None:
                    pe.wait_ge(k_exp_done, 2 * (nb + 1))
                    for t in range(NT):
                        for g in range(2):
                            last_ = nc.tensor.transpose(k_tok_ps[:, t, g * CH:(g + 1) * CH], k_exp[:, g, t * P:(t + 1) * P],
                                                        ident[0:CH, 0:CH])
                    last_.then_inc(k_tok_done, 1)
                if m is not None:
                    if pair is None:
                        scores(0)
                    scores(1)
                if b is not None:
                    pe.wait_ge(k_tok_copied, nb + 1)
                    pe.wait_ge(v_copied, 2 * (nb + 1))
                    for g in range(2):
                        h = slice(g * CH, (g + 1) * CH)
                        for t in range(NT):
                            last_ = nc.tensor.matmul(kv_ps[:, g, :], v_tok[:, t, h], k_tok[:, t, h],
                                                     start=(t == 0), stop=(t == NT - 1))
                    last_.then_inc(kv_done, 1)
                if m is not None:
                    scores(2)
                if b is not None:
                    pe.wait_ge(kv_masked, nb + 1)
                    for g in range(2):
                        last_ = nc.tensor.matmul(mix_ps[:, g, :], kv[:, g, :], wp_ext[:, g, :], start=True, stop=True)
                    last_.then_inc(mix_done, 1)
                    pe.wait_ge(q_norm_done, nb + 1)
                    for g in range(2):
                        query_transposes(g)
                if pair is not None:
                    pe.wait_ge(coef_done, pair + 1)
                    for i in range(2):
                        transposes(coef_ps[i], [coef_split[:, i * NT + t, :] for t in range(NT)], P).then_inc(coef_t_done, 1)
                if b is not None:
                    pe.wait_ge(q_ch_copied, 2 * (nb + 1))
                    pe.wait_ge(mix_ready, 2 * (nb + 1))
                    if n is not None:
                        pe.wait_ge(h_copied, NT * (nn + 1))
                    mixed(0)
                    mixed(1)
                if m is not None:
                    wait_first(pe, seg_exp_done, nm + 1)
                    for t in range(NT):
                        last_ = nc.tensor.transpose(seg_pt_ps[:, t, :], seg_p[:, t, :], ident[:, :])
                    last_.then_inc(seg_pt_done, 1)
                if pair is not None:
                    pe.wait_ge(coef_t_copied, 2 * pair + 2)
                    if b is not None:
                        pe.wait_ge(mix_ready, 2 * (nb + 1))
                    for t in range(2 * NT):
                        last_ = nc.tensor.matmul(ffn_ps[:, t, :], coef_t[:, t // NT, t % NT * P:(t % NT + 1) * P], w_out_split[:, :],
                                                 start=True, stop=True)
                    last_.then_inc(ffn_done, 1)
                if b is not None:
                    mixed(2)

            schedule(pe, slot)

    return nc


_INS = ["x", "L0_attn_Wq", "L0_attn_bq", "L0_attn_Wk", "L0_attn_bk", "L0_attn_Wv", "L0_attn_bv", "L0_attn_Wp",
        "L0_attn_bp", "L0_ffn_weights_in", "L0_ffn_weights_out"]


def kernel(**inputs):
    import numpy as _np
    import concourse.bacc as _bacc
    from concourse import mybir as _mybir
    from concourse.bass_utils import run_bass_kernel_spmd as _run

    nc = _bacc.Bacc("TRN2", target_bir_lowering=False, num_devices=1)
    arrays, args = {}, []
    for name in _INS:
        a = _np.ascontiguousarray(inputs[name])
        arrays[f"in_{name}_dram"] = a
        args.append(nc.dram_tensor(f"in_{name}_dram", a.shape, _mybir.dt.from_np(a.dtype), kind="ExternalInput").ap())
    batches, rows, width = inputs["x"].shape
    tokens = -(-rows // 128) * 64
    args.append(nc.dram_tensor("out_0_dram", (batches, tokens, width), _mybir.dt.float32, kind="ExternalOutput").ap())
    audio_tower_kernel(nc, *args)
    r = _run(nc, [arrays], core_ids=[0])
    return r.results[0]["out_0_dram"]
```

```python
import concourse.bass as bass
from concourse import mybir
from contextlib import ExitStack


def audio_tower_kernel(nc, x, Wq, bq, Wk, bk, Wv, bv, Wp, bp, W_in, W_out, out):
    F32, F32R = mybir.dt.float32, mybir.dt.float32r
    ALU = mybir.AluOpType
    ACT = mybir.ActivationFunctionType
    AX = mybir.AxisListType

    NBATCH, ROWS, D = x.shape
    SEGMENT, DILATION = 128, 2
    SEGTOK = SEGMENT // DILATION
    NTOK = -(-ROWS // SEGMENT) * SEGTOK
    P = 128
    NT = NTOK // P
    LAST = (ROWS - (NT - 1) * P * DILATION + DILATION - 1) // DILATION
    HD = 16
    HEADS = D // HD
    CH = D // 2
    GH = CH // HD
    NODES = W_in.shape[0]
    XD = D + NODES
    LEAVES = 32
    PAIRS = NBATCH // 2
    BANK = 512
    PAD = 256
    SCALE = float(D) ** -0.5
    EPS = 1e-5
    TREE_STEPS = 11
    A0 = 128
    B0 = D - A0
    CONSTANTS = 12
    STEPS_AT_END = 5.0

    ctx = ExitStack()
    with ctx:
        def sb(name, shape, dt=F32):
            return ctx.enter_context(nc.sbuf_tensor(name, shape, dt))

        def sem(name):
            return ctx.enter_context(nc.semaphore(name))

        ident = sb("ident", [P, P])
        head_mask = sb("head_mask", [CH, CH])
        w_nat = sb("w_nat", [CH, 3, 2, 2 * A0])
        w_hi = sb("w_hi", [P, 2, 3 * D], F32R)
        w_lo = sb("w_lo", [P, 2, 3 * D], F32R)
        wp_nat = sb("wp_nat", [CH, 2, D])
        wp_ext = sb("wp_ext", [CH, 2, XD])
        w_in = sb("w_in", [NODES, D])
        w_in_sum = sb("w_in_sum", [NODES, 1])
        w_in_mean = sb("w_in_mean", [NODES, 1])
        w_in_c = sb("w_in_c", [NODES, D])
        router = sb("router", [CH, 2, NODES])
        bq_raw = sb("bq_raw", [P, D])
        bq_round = sb("bq_round", [P, D], F32R)
        bk_col = sb("bk_col", [CH, 2])
        bv_col = sb("bv_col", [CH, 2])
        bp_col = sb("bp_col", [CH, 2])
        bp_row = sb("bp_row", [1, XD])
        head_share = sb("head_share", [1, CH])
        bv_diag = sb("bv_diag", [CH, 2, CH])
        m_const = sb("m_const", [CH, 2, XD])
        w_out_raw = sb("w_out_raw", [P, D])
        w_out_round = sb("w_out_round", [P, D], F32R)
        w_out_split = sb("w_out_split", [P, D], F32R)
        minus_half = sb("minus_half", [P, NT])

        x_tok = [sb(f"x_tok{i}", [P, NT, XD + 1]) for i in range(2)]
        x_ch = sb("x_ch", [CH, 2, NT, P + NODES])
        s_max = sb("s_max", [P, NT])
        seg_p = sb("seg_p", [P, NT, SEGTOK])
        seg_pt = sb("seg_pt", [P, NT, P])
        seg_rz = sb("seg_rz", [P, NT])
        h_ext = [sb(f"h_ext{i}", [P, NT, XD]) for i in range(2)]
        stats1 = sb("stats1", [P, NT, 6])
        moments1 = sb("moments1", [P, NT, 2])
        var1 = sb("var1", [P, NT])
        rstd1 = sb("rstd1", [P, NT])
        y = sb("y", [P, NT, 2 * A0])
        yt = sb("yt", [P, 4, NT * P], F32R)
        k_max = sb("k_max", [CH, 2])
        k_neg = sb("k_neg", [CH, 2])
        k_shift = sb("k_shift", [CH, 2])
        k_exp = sb("k_exp", [CH, 2, NT * P])
        k_sum = sb("k_sum", [CH, 2])
        k_rsum = sb("k_rsum", [CH, 2])
        k_tok = sb("k_tok", [P, NT, D])
        v_tok = sb("v_tok", [P, NT, D])
        q_max = sb("q_max", [P, NT, HEADS])
        q_exp = sb("q_exp", [P, NT, D])
        q_sum = sb("q_sum", [P, NT, HEADS])
        q_rsum = sb("q_rsum", [P, NT, HEADS])
        q_norm = sb("q_norm", [P, NT, D])
        q_ch = sb("q_ch", [CH, 2, NT * P])
        kv = sb("kv", [CH, 2, CH])
        mix = sb("mix", [CH, 2, XD])
        h2_ext = sb("h2_ext", [P, 2, NT, XD])
        stats2 = sb("stats2", [P, NT, 6])
        moments2 = sb("moments2", [P, NT, 2])
        var2 = sb("var2", [P, NT])
        rstd2 = sb("rstd2", [P, NT])
        logits = sb("logits", [P, 2, NT, NODES])
        gelu = sb("gelu", [P, 2 * NT, NODES])
        reach = sb("reach", [P, 2 * NT, NODES])
        tail1 = sb("tail1", [P, 2 * NT])
        tail2 = sb("tail2", [P, 2 * NT])
        coef = sb("coef", [P, 2 * NT, LEAVES])
        coef_split = sb("coef_split", [P, 2 * NT, 4 * LEAVES])
        coef_t = sb("coef_t", [P, 2, NT * P], F32R)
        kept = sb("kept", [P, NT, D])
        result = sb("result", [P, 2 * NT, D])

        psum = ctx.enter_context(nc.psum_tensor("psum", [P, 8 * BANK], F32))

        def bank(b, n=1):
            return psum[:, b * BANK:(b + n) * BANK]

        def tiles_in(b, width):
            return bank(b, 2).rearrange("p (t c) -> p t c", c=PAD)[:, 0:NT, 0:width]

        yt_ps = [bank(b) for b in (5, 0)]
        x_ch_ps = [bank(6 + c) for c in range(2)]
        k_ps = [bank(3 + c) for c in range(2)]
        qv_ps = bank(5, 3).rearrange("p (t c) -> p t c", c=BANK)
        SW = P + NODES
        s_ps = bank(0)[:, 0:NT * SW].rearrange("p (t c) -> p t c", c=SW)
        coef_ps = [bank(b) for b in (6, 7)]
        k_tok_ps = bank(3, 2).rearrange("p (g x) -> p g x", x=BANK)[:, :, 0:NT * CH].rearrange("p g (t c) -> p t g c", c=CH)
        seg_pt_ps = bank(0)[0:SEGTOK, 0:NT * P].rearrange("p (t c) -> p t c", c=P)
        kv_ps = bank(5)[0:CH, 0:2 * CH].rearrange("p (g c) -> p g c", c=CH)
        ffn_ps = bank(5, 3).rearrange("p (t c) -> p t c", c=PAD)[:, :, 0:D]
        h_ps = tiles_in(1, XD + 1)
        q_ch_ps = [bank(3 + c) for c in range(2)]
        mix_ps = bank(5)[0:CH, 0:2 * XD].rearrange("p (g c) -> p g c", c=XD)
        out_ps = tiles_in(1, XD)

        w_ps = bank(3, 3).rearrange("p (m c) -> p m c", c=BANK)[:, :, 0:2 * D].rearrange("p m (a o) -> p a m o", a=2)
        wp_ps = bank(2)[0:CH, 0:2 * D].rearrange("p (g c) -> p g c", g=2)
        router_ps = bank(0)[0:CH, 0:2 * NODES].rearrange("p (g n) -> p g n", g=2)
        wp_router_ps = bank(1)[0:CH, 0:2 * NODES].rearrange("p (g n) -> p g n", g=2)
        bp_router_ps = bank(1)[0:1, 2 * NODES:3 * NODES]
        m_const_ps = bank(2)[0:CH, 0:2 * XD].rearrange("p (g c) -> p g c", g=2)

        ident_built, const_built, tiles_cleared = sem("ident_built"), sem("const_built"), sem("tiles_cleared")
        w_in_loaded, w_loaded, wp_loaded = sem("w_in_loaded"), sem("w_loaded"), sem("wp_loaded")
        biases_loaded, w_out_loaded = sem("biases_loaded"), sem("w_out_loaded")
        w_transposed, wp_transposed, router_transposed = sem("w_transposed"), sem("wp_transposed"), sem("router_transposed")
        w_in_centred, router_ready, w_high_done = sem("w_in_centred"), sem("router_ready"), sem("w_high_done")
        wp_router_done, setup_dve = sem("wp_router_done"), sem("setup_dve")
        wp_ready, m_const_done, const_ready = sem("wp_ready"), sem("m_const_done"), sem("const_ready")
        x_loaded = [sem("x_loaded0"), sem("x_loaded1")]
        x_ch_done, x_ch_copied = sem("x_ch_done"), sem("x_ch_copied")
        s_done, s_max_done, x_router_copied, s_shifted = sem("s_done"), sem("s_max_done"), sem("x_router_copied"), sem("s_shifted")
        seg_exp_done, seg_pt_done, seg_pt_copied = sem("seg_exp_done"), sem("seg_pt_done"), sem("seg_pt_copied")
        h_done, seg_rz_done, h_copied = sem("h_done"), sem("seg_rz_done"), sem("h_copied")
        stats1_done, moments1_done, var1_done, rstd1_done = sem("stats1_done"), sem("moments1_done"), sem("var1_done"), sem("rstd1_done")
        y_done, y_twice_done = sem("y_done"), sem("y_twice_done")
        yt_done, yt_high_done = sem("yt_done"), sem("yt_high_done")
        yt_low_done = sem("yt_low_done")
        k_done, k_max_done, k_neg_done, k_shift_done = sem("k_done"), sem("k_max_done"), sem("k_neg_done"), sem("k_shift_done")
        k_exp_done, k_tok_done, k_tok_copied, k_rsum_done = sem("k_exp_done"), sem("k_tok_done"), sem("k_tok_copied"), sem("k_rsum_done")
        qv_done, v_copied = sem("qv_done"), sem("v_copied")
        q_max_done, q_shifted, q_exp_done, q_sum_done, q_rsum_done, q_norm0_done, q_norm1_done = (
            sem("q_max_done"), sem("q_shifted"), sem("q_exp_done"), sem("q_sum_done"), sem("q_rsum_done"), sem("q_norm0_done"), sem("q_norm1_done"))
        q_ch_done, q_ch_copied = sem("q_ch_done"), sem("q_ch_copied")
        kv_done, kv_masked, mix_done, mix_ready = sem("kv_done"), sem("kv_masked"), sem("mix_done"), sem("mix_ready")
        out_done, h2_done = sem("out_done"), sem("h2_done")
        stats2_done, moments2_done, var2_done, rstd2_done, logits_done = (
            sem("stats2_done"), sem("moments2_done"), sem("var2_done"), sem("rstd2_done"), sem("logits_done"))
        gelu_done, coef_high_done, coef_done = sem("gelu_done"), sem("coef_high_done"), sem("coef_done")
        tree_step = sem("tree_step")
        coef_t_done, coef_t_copied, ffn_done, result_done = sem("coef_t_done"), sem("coef_t_copied"), sem("ffn_done"), sem("result_done")
        wait_passed = sem("wait_passed")
        tokens_kept = sem("tokens_kept")
        stored = sem("stored")

        def wait(eng, semaphore, count):
            if not (isinstance(count, int) and count <= 0):
                eng.wait_ge(semaphore, count)

        def wait_first(eng, semaphore, count):
            eng.wait_ge(semaphore, count)
            eng.nop().then_inc(wait_passed, 1)

        def schedule(eng, slot, looped=PAIRS - 1):
            slot(None, None, (0, 0), None)
            slot(None, (0, 0), (0, 1), None)
            slot((0, 0), (0, 1), (1, 0), None)
            slot((0, 1), (1, 0), (1, 1), None)
            slot((1, 0), (1, 1), (2, 0), 0)
            slot((1, 1), (2, 0), (2, 1), 0)
            with eng.Fori(2, looped) as j:
                slot((j, 0), (j, 1), (j + 1, 0), j - 1)
                slot((j, 1), (j + 1, 0), (j + 1, 1), j - 1)
            for j in range(looped, PAIRS - 1):
                slot((j, 0), (j, 1), (j + 1, 0), j - 1)
                slot((j, 1), (j + 1, 0), (j + 1, 1), j - 1)
            last = PAIRS - 1
            slot((last, 0), (last, 1), None, last - 1)
            slot((last, 1), None, None, last - 1)
            slot(None, None, None, last)

        def stages(b, pair):
            tree = pair if b is None or b[1] == 0 else None
            products = pair if b is None or b[1] == 1 else None
            return tree, products

        def number(batch):
            return 2 * batch[0] + batch[1]

        def ended_before(b, pair):
            if b is None:
                return None if pair is None else (PAIRS - 1, 1)
            if b[1] == 1:
                return b[0], 0
            return None if isinstance(b[0], int) and b[0] == 0 else (b[0] - 1, 1)

        def seg_half(s):
            return slice(s * SEGTOK, (s + 1) * SEGTOK)

        def is_first(b):
            return b is not None and isinstance(b[0], int) and number(b) == 0

        def is_ahead(batch):
            return batch[1] == 1

        def next_ahead(m):
            return None if m is None or m[1] == 1 else (m[0], 1)

        def load_weights(eng, m, w):
            rows = w.rearrange("(h o) i -> o h i", h=2)
            eng.dma_start(w_nat[:, m, :, 0:D], rows).then_inc(w_loaded, 16)
            eng.dma_start(w_nat[:, m, :, D:2 * A0], rows[:, :, A0:D]).then_inc(w_loaded, 16)

        def normalise_queries(vec, g):
            h = slice(g * CH, (g + 1) * CH)
            return vec.tensor_tensor(q_norm[:, :, h].rearrange("p t (h c) -> p t h c", c=HD),
                                     q_exp[:, :, h].rearrange("p t (h c) -> p t h c", c=HD),
                                     q_rsum[:, :, g * GH:(g + 1) * GH].unsqueeze(3).to_broadcast([P, NT, GH, HD]), ALU.mult)

        coef4 = coef_split[:, :, :].bitcast(F32R).rearrange("p t (s e l) -> p t s e l", e=2, l=LEAVES)
        coef4_f = coef_split[:, :, :].rearrange("p t (s e l) -> p t s e l", e=2, l=LEAVES)
        coef_twice = coef[:, :, :].unsqueeze(2).to_broadcast([P, 2 * NT, 2, LEAVES])

        block = ctx.enter_context(nc.Block())

        @block.sync
        def _(sp):
            def load_x(batch):
                p = batch[1]
                rows = x[bass.ds(number(batch), 1), :, :].rearrange("a r c -> (a r) c")
                whole = rows[0:(NT - 1) * P * DILATION, :].rearrange("(t q s) c -> q t s c", q=P, s=DILATION)
                sp.dma_start(x_tok[p][:, 0:NT - 1, 0:D], whole[:, :, 0, :]).then_inc(x_loaded[p], 16)
                rest = rows[(NT - 1) * P * DILATION:ROWS, :].rearrange("(q s) c -> q s c", s=DILATION)
                sp.dma_start(x_tok[p][0:LAST, NT - 1, 0:D], rest[:, 0, :]).then_inc(x_loaded[p], 16)

            sp.dma_start(w_in[:, :], W_in).then_inc(w_in_loaded, 16)
            sp.wait_ge(tiles_cleared, 2)
            load_x((0, 0))
            load_weights(sp, 2, Wk)
            sp.dma_start(wp_nat[:, :, :], Wp.rearrange("(h o) i -> o h i", h=2)).then_inc(wp_loaded, 16)
            for col, b in ((bp_col, bp), (bv_col, bv), (bk_col, bk)):
                sp.dma_start(col[:, :], b.rearrange("(g c) -> c g", g=2),
                             allow_slow_non_contiguous=True).then_inc(biases_loaded, 16)
            sp.dma_start(bp_row[0:1, 0:D], bp.rearrange("(a c) -> a c", a=1)).then_inc(biases_loaded, 16)
            load_x((0, 1))
            sp.wait_ge(tiles_cleared, 4)
            for part in (64, 96):
                sp.dma_start(bq_raw[part:part + 1, :], bq.rearrange("(a c) -> a c", a=1)).then_inc(biases_loaded, 16)
            first = NODES // 2
            for s in range(4):
                at = s * LEAVES
                sp.dma_start(w_out_raw[at:at + NODES - 1, :], W_out[1:NODES, :]).then_inc(w_out_loaded, 16)
                sp.dma_start(w_out_raw[at + NODES - 1:at + NODES - 1 + NODES - first, :],
                             W_out[NODES - 1:NODES, :].to_broadcast([NODES - first, D])).then_inc(w_out_loaded, 16)

            def store(pair):
                parts = 2 if isinstance(pair, int) and pair == PAIRS - 1 else 1
                for i in range(parts):
                    sp.wait_ge(result_done, 2 * pair + (i + 1) * 2 // parts)
                    dst = out[bass.ds(2 * pair + i, 2 // parts), :, :].rearrange("a (t q) c -> q (a t) c", q=P)
                    sp.dma_start(dst, result[:, i * NT:i * NT + 2 * NT // parts, :]).then_inc(stored, 16)

            def slot(b, n, m, pair):
                if n is not None and not (isinstance(n[0], int) and n[0] + 1 >= PAIRS):
                    sp.wait_ge(h_done, number(n) + 1)
                    load_x((n[0] + 1, n[1]))
                if stages(b, pair)[1] is not None:
                    store(pair)

            schedule(sp, slot, looped=PAIRS - 2)
            sp.wait_ge(stored, 16 * (PAIRS + 1))

        @block.gpsimd
        def _(pool):
            for i in range(2):
                nc.gpsimd.memset(x_tok[i][:, NT - 1, 0:D], 0.0).then_inc(tiles_cleared, 1)
            nc.gpsimd.memset(ident[:, :], 0.0).then_inc(const_built, 1)
            nc.gpsimd.memset(head_mask[:, :], float(HD) ** -0.5).then_inc(const_built, 1)
            pool.wait_ge(const_built, 2)
            nc.gpsimd.affine_select(out=ident[:, :], in_=ident[:, :], compare_op=ALU.not_equal, fill=1.0,
                                    base=0, pattern=[[-1, P]], channel_multiplier=1).then_inc(ident_built, 1)
            nc.gpsimd.memset(bq_raw[:, :], 0.0).then_inc(tiles_cleared, 1)
            nc.gpsimd.memset(w_out_raw[:, :], 0.0).then_inc(tiles_cleared, 1)
            heads = head_mask[:, :].rearrange("p (g c) -> p g c", c=HD)
            nc.gpsimd.affine_select(out=heads, in_=heads, compare_op=ALU.is_ge, fill=0.0, base=0,
                                    pattern=[[-HD, GH], [0, HD]], channel_multiplier=1).then_inc(const_built, 1)
            pool.wait_ge(const_built, 3)
            nc.gpsimd.affine_select(out=heads, in_=heads, compare_op=ALU.is_ge, fill=0.0, base=HD - 1,
                                    pattern=[[HD, GH], [0, HD]], channel_multiplier=-1).then_inc(const_built, 1)
            nc.gpsimd.memset(seg_pt[:, :, :], 0.0).then_inc(const_built, 1)
            for i in range(2):
                nc.gpsimd.memset(x_tok[i][:, :, XD:XD + 1], 1.0).then_inc(const_built, 1)
            nc.gpsimd.memset(yt[:, 3, :].bitcast(F32), 1.0).then_inc(const_built, 1)
            nc.gpsimd.memset(w_lo[:, 1, :].bitcast(F32), 0.0).then_inc(const_built, 1)
            nc.gpsimd.memset(head_share[:, :], 1.0 / HEADS).then_inc(const_built, 1)
            nc.gpsimd.memset(minus_half[:, :], -0.5).then_inc(const_built, 1)
            nc.gpsimd.memset(coef[:, :, :], 0.0).then_inc(const_built, 1)
            pool.wait_ge(const_built, CONSTANTS)

            HALF = NODES // 2
            flat_logits = logits[:, :, :, :].rearrange("p b t n -> p (b t) n")

            def step(pair, k, instruction):
                instruction.then_inc(tree_step, 1)
                wait_first(pool, tree_step, pair * TREE_STEPS + k)

            def twice(a):
                return a.unsqueeze(3).to_broadcast([P, 2 * NT, a.shape[2], 2])

            child = reach[:, :, 1:NODES].rearrange("p t (n c) -> p t n c", c=2)

            def tree_paths(pair):
                wait_first(pool, logits_done, 2 * pair + 2)
                nc.gpsimd.tensor_scalar(child[:, :, :, 1], flat_logits[:, :, 0:HALF], 0.0, None, ALU.is_gt)
                step(pair, 1, nc.gpsimd.tensor_scalar(child[:, :, :, 0], flat_logits[:, :, 0:HALF], 0.0, None, ALU.is_le))
                for k, (lo, hi) in enumerate(((3, 7), (7, 15), (15, NODES))):
                    kids = reach[:, :, lo:hi].rearrange("p t (n c) -> p t n c", c=2)
                    step(pair, 2 + k, nc.gpsimd.tensor_tensor(kids, kids, twice(reach[:, :, (lo - 1) // 2:(hi - 1) // 2]), ALU.mult))
                step(pair, 5, nc.gpsimd.tensor_tensor(tail1[:, :], reach[:, :, HALF], reach[:, :, 5], ALU.add))
                step(pair, 6, nc.gpsimd.tensor_tensor(tail2[:, :], tail1[:, :], reach[:, :, 6], ALU.add))

            def tree_coefficients(pair):
                pool.wait_ge(gelu_done, pair + 1)
                wait(pool, coef_done, pair)
                head = coef[:, :, 0:NODES - 1].rearrange("p t (n c) -> p t n c", c=2)
                step(pair, 7, nc.gpsimd.tensor_tensor(head, child, twice(gelu[:, :, 0:HALF]), ALU.mult))
                step(pair, 8, nc.gpsimd.tensor_tensor(reach[:, :, NODES - 1], reach[:, :, NODES - 1], tail2[:, :], ALU.add))
                step(pair, 9, nc.gpsimd.tensor_tensor(coef[:, :, NODES - 1:NODES - 1 + NODES - HALF], reach[:, :, HALF:NODES],
                                                      gelu[:, :, HALF:NODES], ALU.mult))
                step(pair, 10, nc.gpsimd.tensor_scalar(tail1[:, :], gelu[:, :, NODES - 1], STEPS_AT_END, None, ALU.mult))
                step(pair, 11, nc.gpsimd.tensor_tensor(coef[:, :, LEAVES - 2], coef[:, :, LEAVES - 2], tail1[:, :], ALU.add))

            def second_moments(b):
                wait_first(pool, moments2_done, NT * (number(b) + 1))
                nc.gpsimd.tensor_scalar(var2[:, :], moments2[:, :, 1], EPS, None, ALU.add).then_inc(var2_done, 1)
                pool.wait_ge(var2_done, number(b) + 1)
                nc.gpsimd.tensor_tensor(rstd2[:, :], var2[:, :], minus_half[:, :], ALU.pow).then_inc(rstd2_done, 1)
                pool.wait_ge(rstd2_done, number(b) + 1)
                wait(pool, gelu_done, b[0])
                nc.gpsimd.tensor_tensor(logits[:, b[1], :, :], h2_ext[:, b[1], :, D:XD],
                                        rstd2[:, :].unsqueeze(2).to_broadcast([P, NT, NODES]),
                                        ALU.mult).then_inc(logits_done, 1)

            def slot(b, n, m, pair):
                tree, _ = stages(b, pair)
                if tree is not None:
                    wait_first(pool, h2_done, 2 * (2 * tree + 1))
                    if not (isinstance(tree, int) and tree == 0):
                        wait_first(pool, result_done, 2 * tree)
                    nc.gpsimd.tensor_copy(kept[:, :, :], h2_ext[:, 0, :, 0:D]).then_inc(tokens_kept, 1)
                ended = ended_before(b, pair)
                if ended is not None:
                    second_moments(ended)
                if tree is not None:
                    tree_paths(tree)
                if n is not None:
                    wait_first(pool, moments1_done, NT * (number(n) + 1))
                    nc.gpsimd.tensor_scalar(var1[:, :], moments1[:, :, 1], EPS, None, ALU.add).then_inc(var1_done, 1)
                    pool.wait_ge(var1_done, number(n) + 1)
                    nc.gpsimd.tensor_tensor(rstd1[:, :], var1[:, :], minus_half[:, :], ALU.pow).then_inc(rstd1_done, 1)
                if b is not None:
                    pool.wait_ge(q_rsum_done, number(b) + 1)
                    wait(pool, q_ch_done, 2 * number(b))
                    normalise_queries(nc.gpsimd, 1).then_inc(q_norm1_done, 1)
                if n is not None:
                    wait_first(pool, y_done, NT * (number(n) + 1))
                    nc.gpsimd.tensor_copy(y[:, :, D:2 * A0], y[:, :, A0:D]).then_inc(y_twice_done, 1)
                if tree is not None:
                    tree_coefficients(tree)

            schedule(pool, slot)

        @block.scalar
        def _(act):
            load_weights(act, 0, Wq)
            load_weights(act, 1, Wv)

            def copy_tokens(batch):
                for c in range(2):
                    act.wait_ge(x_ch_done, 2 * number(batch) + c + 1)
                    nc.scalar.activation(x_ch[:, c, :, 0:P],
                                         x_ch_ps[c][0:CH, 0:NT * P].rearrange("p (t c) -> p t c", c=P),
                                         ACT.Copy).then_inc(x_ch_copied, 1)

            def coefficients_high(pair):
                act.wait_ge(tree_step, TREE_STEPS * (pair + 1))
                nc.scalar.activation(coef4[:, :, :, 0, :], coef_twice, ACT.Copy).then_inc(coef_high_done, 1)

            def slot(b, n, m, pair):
                tree, products = stages(b, pair)
                if b is not None:
                    for c in range(2):
                        act.wait_ge(yt_done, 2 * number(b) + c + 1)
                        nc.scalar.activation(yt[:, c, :], yt_ps[c][:, 0:NT * P], ACT.Copy).then_inc(yt_high_done, 1)
                    nc.scalar.activation(yt[0:B0, 3, :], yt_ps[1][0:B0, 0:NT * P], ACT.Copy).then_inc(yt_high_done, 1)
                if m is not None and not is_ahead(m):
                    copy_tokens(m)
                if n is not None:
                    act.wait_ge(seg_rz_done, number(n) + 1)
                    for t in range(NT):
                        nc.scalar.activation(h_ext[n[1]][:, t, :], h_ps[:, t, 0:XD], ACT.Copy,
                                             scale=seg_rz[:, t:t + 1]).then_inc(h_copied, 1)
                if products is not None and b is not None:
                    coefficients_high(pair)
                if b is not None:
                    act.wait_ge(k_shift_done, number(b) + 1)
                    for g in range(2):
                        nc.scalar.activation(k_exp[:, g, :], k_ps[g][0:CH, 0:NT * P], ACT.Exp,
                                             bias=k_shift[:, g:g + 1],
                                             accum_out=k_sum[:, g:g + 1]).then_inc(k_exp_done, 1)
                    act.wait_ge(q_shifted, NT * number(b) + NT - 1)
                    nc.scalar.activation(v_tok[:, 0:NT - 1, :], qv_ps[:, 0:NT - 1, D:2 * D], ACT.Copy).then_inc(v_copied, 1)
                    act.wait_ge(k_tok_done, number(b) + 1)
                    nc.scalar.activation(k_tok[:, :, :].rearrange("p t (g c) -> p t g c", c=CH), k_tok_ps,
                                         ACT.Copy).then_inc(k_tok_copied, 1)
                    act.wait_ge(q_shifted, NT * (number(b) + 1))
                    nc.scalar.activation(v_tok[:, NT - 1, :], qv_ps[:, NT - 1, D:2 * D], ACT.Copy).then_inc(v_copied, 1)
                    nc.scalar.activation(q_exp[:, :, :], q_exp[:, :, :], ACT.Exp).then_inc(q_exp_done, 1)
                if tree is not None:
                    act.wait_ge(logits_done, 2 * pair + 2)
                    nc.scalar.activation(gelu[:, :, :], logits[:, :, :, :].rearrange("p b t n -> p (b t) n"),
                                         ACT.Gelu).then_inc(gelu_done, 1)
                if products is not None and b is None:
                    coefficients_high(pair)
                if b is not None:
                    for g in range(2):
                        act.wait_ge(q_ch_done, 2 * number(b) + g + 1)
                        nc.scalar.activation(q_ch[:, g, :], q_ch_ps[g][0:CH, 0:NT * P], ACT.Copy).then_inc(q_ch_copied, 1)
                if products is not None:
                    for i in range(2):
                        act.wait_ge(coef_t_done, 2 * pair + i + 1)
                        nc.scalar.activation(coef_t[:, i, :], coef_ps[i][:, 0:NT * P], ACT.Copy).then_inc(coef_t_copied, 1)
                if m is not None:
                    act.wait_ge(s_shifted, 2 * (number(m) + 1))
                    nc.scalar.activation(seg_p[:, :, :], seg_p[:, :, :], ACT.Exp, scale=SCALE).then_inc(seg_exp_done, 1)
                if next_ahead(m) is not None and n is not None:
                    copy_tokens(next_ahead(m))
                if m is not None:
                    if n is None:
                        act.wait_ge(const_built, CONSTANTS)
                    act.wait_ge(seg_pt_done, number(m) + 1)
                    for s in range(2):
                        h = seg_half(s)
                        nc.scalar.activation(seg_pt[h, :, h], seg_pt_ps[:, :, h], ACT.Copy).then_inc(seg_pt_copied, 1)
                if next_ahead(m) is not None and n is None:
                    copy_tokens(next_ahead(m))
                if n is None and m is not None:
                    act.wait_ge(w_transposed, 1)
                    for a in range(2):
                        nc.scalar.activation(w_hi[:, a, :].rearrange("p (m o) -> p m o", m=3), w_ps[:, a],
                                             ACT.Copy).then_inc(w_high_done, 1)

            schedule(act, slot)

        @block.vector
        def _(dve):
            steps = [0]

            def step(instruction):
                steps[0] += 1
                instruction.then_inc(setup_dve, 1)
                dve.wait_ge(setup_dve, steps[0])

            dve.wait_ge(w_in_loaded, 16)
            step(nc.vector.tensor_reduce(w_in_sum[:, :], w_in[:, :], AX.X, ALU.add))
            step(nc.vector.tensor_scalar(w_in_mean[:, :], w_in_sum[:, :], 1.0 / D, None, ALU.mult))
            nc.vector.tensor_scalar(w_in_c[:, :], w_in[:, :], w_in_mean[:, 0:1], None, ALU.subtract).then_inc(w_in_centred, 1)
            dve.wait_ge(router_transposed, 1)
            nc.vector.tensor_copy(x_ch[:, :, :, P:P + NODES],
                                  router_ps.unsqueeze(2).to_broadcast([CH, 2, NT, NODES])).then_inc(router_ready, 1)
            nc.vector.tensor_copy(router[:, :, :], router_ps).then_inc(router_ready, 1)

            def split_weights():
                dve.wait_ge(w_high_done, 2)
                for a, rows in ((0, A0), (1, B0)):
                    step(nc.vector.tensor_tensor(w_lo[0:rows, a, :].rearrange("p (m o) -> p m o", m=3), w_ps[0:rows, a],
                                                 w_hi[0:rows, a, :].bitcast(F32).rearrange("p (m o) -> p m o", m=3), ALU.subtract))
                nc.vector.nop().then_inc(const_ready, 1)

            def extend_projection():
                dve.wait_ge(const_built, CONSTANTS)
                dve.wait_ge(wp_transposed, 1)
                step(nc.vector.tensor_copy(wp_ext[:, :, 0:D], wp_ps))
                dve.wait_ge(wp_router_done, 1)
                step(nc.vector.tensor_copy(wp_ext[:, :, D:XD], wp_router_ps))
                dve.wait_ge(biases_loaded, 16 * 6)
                step(nc.vector.tensor_copy(bp_row[0:1, D:XD], bp_router_ps))
                for g in range(2):
                    step(nc.vector.tensor_scalar(bv_diag[:, g, :], head_mask[:, :], bv_col[:, g:g + 1], None, ALU.mult))
                nc.vector.nop().then_inc(wp_ready, 1)

            def split_query_bias():
                dve.wait_ge(biases_loaded, 16 * 6)
                dve.wait_ge(const_built, CONSTANTS)
                step(nc.vector.tensor_copy(bq_round[B0:P, :], bq_raw[B0:P, :]))
                step(nc.vector.tensor_copy(w_lo[64:96, 1, 0:D], bq_round[64:96, :].bitcast(F32)))
                step(nc.vector.tensor_tensor(w_lo[96:P, 1, 0:D], bq_raw[96:P, :], bq_round[96:P, :].bitcast(F32), ALU.subtract))

            def split_w_out():
                dve.wait_ge(w_out_loaded, 16 * 8)
                step(nc.vector.tensor_copy(w_out_round[:, :], w_out_raw[:, :]))
                step(nc.vector.tensor_copy(w_out_split[0:64, :], w_out_round[0:64, :].bitcast(F32)))
                step(nc.vector.tensor_tensor(w_out_split[64:P, :], w_out_raw[64:P, :], w_out_round[64:P, :].bitcast(F32), ALU.subtract))
                nc.vector.nop().then_inc(const_ready, 1)

            def by_head(a):
                return a.rearrange("p t (h c) -> p t h c", c=HD)

            def bn_statistics(source, stats, stats_done, t):
                nc.vector.bn_stats(stats[:, t, :], source[:, t, 0:D]).then_inc(stats_done, 1)

            def moments(stats, stats_done, result_, result_done_, count):
                wait_first(dve, stats_done, NT * count)
                for t in range(NT):
                    nc.vector.bn_aggr(result_[:, t, :], stats[:, t, :]).then_inc(result_done_, 1)

            def slot(b, n, m, pair):
                nb = None if b is None else number(b)
                nn = None if n is None else number(n)
                _, products = stages(b, pair)
                nm = None if m is None else number(m)

                def add_residual(first, end):
                    dve.wait_ge(out_done, NT * nb + end)
                    nc.vector.tensor_tensor(h2_ext[:, b[1], first:end, :], out_ps[:, first:end, :], h_ext[b[1]][:, first:end, :],
                                            ALU.add).then_inc(h2_done, 1)

                def normalise():
                    dve.wait_ge(rstd1_done, nn + 1)
                    wait(dve, yt_done, 2 * nn)
                    for t in range(NT):
                        nc.vector.tensor_scalar(y[:, t, 0:D], h_ext[n[1]][:, t, 0:D], moments1[:, t, 0:1], rstd1[:, t:t + 1],
                                                ALU.subtract, ALU.mult).then_inc(y_done, 1)

                def shift_scores():
                    dve.wait_ge(s_done, NT * (nm + 1))
                    for s in range(2):
                        h = seg_half(s)
                        nc.vector.tensor_reduce(s_max[h, :], s_ps[h, :, h], AX.X, ALU.max).then_inc(s_max_done, 1)
                    nc.vector.tensor_copy(x_tok[m[1]][:, :, D:XD], s_ps[:, :, P:P + NODES]).then_inc(x_router_copied, 1)
                    dve.wait_ge(s_max_done, 2 * (nm + 1))
                    for s in range(2):
                        h = seg_half(s)
                        nc.vector.tensor_tensor(seg_p[h, :, :], s_ps[h, :, h],
                                                s_max[h, :].unsqueeze(2).to_broadcast([SEGTOK, NT, SEGTOK]),
                                                ALU.subtract).then_inc(s_shifted, 1)

                def query_maxima(t):
                    dve.wait_ge(qv_done, NT * nb + t + 1)
                    nc.vector.tensor_reduce(q_max[:, t, :], qv_ps[:, t, 0:D].rearrange("p (h c) -> p h c", c=HD),
                                            AX.X, ALU.max).then_inc(q_max_done, 1)

                def shift_queries(t):
                    dve.wait_ge(q_max_done, NT * nb + t + 1)
                    nc.vector.tensor_tensor(q_exp[:, t, :].rearrange("p (h c) -> p h c", c=HD),
                                            qv_ps[:, t, 0:D].rearrange("p (h c) -> p h c", c=HD),
                                            q_max[:, t, :].unsqueeze(2).to_broadcast([P, HEADS, HD]),
                                            ALU.subtract).then_inc(q_shifted, 1)

                if b is not None:
                    dve.wait_ge(yt_high_done, 3 * nb + 1)
                    nc.vector.tensor_tensor(yt[:, 2, :], yt_ps[0][:, 0:NT * P], yt[:, 0, :].bitcast(F32),
                                            ALU.subtract).then_inc(yt_low_done, 1)
                    dve.wait_ge(yt_high_done, 3 * nb + 2)
                    low = yt[B0:P, 1, :]
                    nc.vector.tensor_tensor(low, yt_ps[1][B0:P, 0:NT * P], low.bitcast(F32), ALU.subtract).then_inc(yt_low_done, 1)
                if n is not None:
                    dve.wait_ge(h_done, nn + 1)
                    nc.vector.reciprocal(seg_rz[:, :], h_ps[:, :, XD]).then_inc(seg_rz_done, 1)
                ended = ended_before(b, pair)
                if ended is not None:
                    dve.wait_ge(h2_done, 2 * (number(ended) + 1))
                    for t in range(NT):
                        bn_statistics(h2_ext[:, ended[1]], stats2, stats2_done, t)
                    moments(stats2, stats2_done, moments2, moments2_done, number(ended) + 1)
                if b is not None:
                    for g in range(2):
                        dve.wait_ge(k_done, 2 * nb + g + 1)
                        nc.vector.tensor_reduce(k_max[:, g:g + 1], k_ps[g][0:CH, 0:NT * P], AX.X, ALU.max).then_inc(k_max_done, 1)
                    dve.wait_ge(k_max_done, 2 * (nb + 1))
                    nc.vector.scalar_tensor_tensor(k_neg[:, :], k_max[:, :], -1.0, bk_col[:, :],
                                                   ALU.mult, ALU.subtract).then_inc(k_neg_done, 1)
                    dve.wait_ge(k_neg_done, nb + 1)
                    nc.vector.tensor_tensor(k_shift[:, :], k_neg[:, :], bk_col[:, :], ALU.add).then_inc(k_shift_done, 1)
                    wait(dve, q_norm0_done, nb)
                    wait(dve, q_norm1_done, nb)
                    query_maxima(0)
                    query_maxima(1)
                    shift_queries(0)
                    shift_queries(1)
                    query_maxima(2)
                if b is None and n is not None:
                    split_query_bias()
                if n is not None:
                    dve.wait_ge(h_copied, NT * (nn + 1))
                    bn_statistics(h_ext[n[1]], stats1, stats1_done, 0)
                if b is not None:
                    shift_queries(2)
                if n is not None:
                    bn_statistics(h_ext[n[1]], stats1, stats1_done, 1)
                    bn_statistics(h_ext[n[1]], stats1, stats1_done, 2)
                    moments(stats1, stats1_done, moments1, moments1_done, nn + 1)
                if b is None and n is not None:
                    shift_scores()
                if b is not None:
                    dve.wait_ge(q_exp_done, nb + 1)
                    nc.vector.tensor_reduce(q_sum[:, :, :], by_head(q_exp[:, :, :]), AX.X, ALU.add).then_inc(q_sum_done, 1)
                    dve.wait_ge(kv_done, nb + 1)
                    nc.vector.tensor_tensor(kv[:, :, :], kv_ps, head_mask[:, :].unsqueeze(1).to_broadcast([CH, 2, CH]),
                                            ALU.mult).then_inc(kv_masked, 1)
                    dve.wait_ge(q_sum_done, nb + 1)
                    nc.vector.reciprocal(q_rsum[:, :, :], q_sum[:, :, :]).then_inc(q_rsum_done, 1)
                    nc.vector.reciprocal(k_rsum[:, :], k_sum[:, :]).then_inc(k_rsum_done, 1)
                    dve.wait_ge(q_rsum_done, nb + 1)
                    wait(dve, q_ch_done, 2 * nb)
                    normalise_queries(nc.vector, 0).then_inc(q_norm0_done, 1)
                if products is not None:
                    dve.wait_ge(coef_high_done, pair + 1)
                    nc.vector.tensor_tensor(coef4[:, :, :, 1, :], coef_twice, coef4_f[:, :, :, 0, :],
                                            ALU.subtract).then_inc(coef_done, 1)
                if n is not None and b is None:
                    normalise()
                if b is None and n is not None:
                    split_weights()
                    extend_projection()
                if is_first(b):
                    dve.wait_ge(m_const_done, 1)
                    step(nc.vector.tensor_copy(m_const[:, :, :], m_const_ps))
                if b is not None:
                    dve.wait_ge(mix_done, nb + 1)
                    dve.wait_ge(k_rsum_done, nb + 1)
                    for g in range(2):
                        nc.vector.scalar_tensor_tensor(mix[:, g, :], mix_ps[:, g, :], k_rsum[:, g:g + 1], m_const[:, g, :],
                                                       ALU.mult, ALU.add).then_inc(mix_ready, 1)
                if m is not None and not (b is None and n is not None):
                    shift_scores()
                if n is not None and b is not None:
                    normalise()
                if products is not None:
                    dve.wait_ge(ffn_done, pair + 1)
                    dve.wait_ge(tokens_kept, pair + 1)
                    wait(dve, stored, pair * 16)
                    nc.vector.tensor_tensor(result[:, 0:NT, :], ffn_ps[:, 0:NT], kept[:, :, :], ALU.add).then_inc(result_done, 1)
                    nc.vector.tensor_tensor(result[:, NT:2 * NT, :], ffn_ps[:, NT:2 * NT], h2_ext[:, 1, :, 0:D],
                                            ALU.add).then_inc(result_done, 1)
                if b is not None:
                    wait(dve, logits_done, nb - 1)
                    if b[1] == 0:
                        wait(dve, tokens_kept, b[0])
                    else:
                        wait(dve, result_done, 2 * b[0])
                    add_residual(0, NT - 1)
                    add_residual(NT - 1, NT)
                if is_first(b):
                    split_w_out()

            schedule(dve, slot)

        @block.tensor
        def _(pe):
            pe.wait_ge(ident_built, 1)
            pe.wait_ge(w_in_centred, 1)
            for g in range(2):
                last = nc.tensor.transpose(router_ps[:, g, :], w_in_c[:, g * CH:(g + 1) * CH], ident[0:NODES, 0:NODES])
            last.then_inc(router_transposed, 1)

            def transpose_weights():
                pe.wait_ge(w_loaded, 16 * 6)
                for i in range(3):
                    for a in range(2):
                        for h in range(2):
                            last_ = nc.tensor.transpose(w_ps[:, a, i, h * CH:(h + 1) * CH],
                                                        w_nat[:, i, h, a * A0:(a + 1) * A0], ident[0:CH, 0:CH])
                last_.then_inc(w_transposed, 1)

            def project_router():
                pe.wait_ge(wp_loaded, 16)
                pe.wait_ge(h_copied, NT)
                for e in range(2):
                    for h in range(2):
                        last_ = nc.tensor.transpose(wp_ps[:, e, h * CH:(h + 1) * CH], wp_nat[:, h, e * CH:(e + 1) * CH],
                                                    ident[0:CH, 0:CH])
                last_.then_inc(wp_transposed, 1)
                pe.wait_ge(biases_loaded, 16 * 6)
                pe.wait_ge(router_ready, 2)
                for e in range(2):
                    for h in range(2):
                        nc.tensor.matmul(wp_router_ps[:, e, :], wp_nat[:, h, e * CH:(e + 1) * CH],
                                         router[:, h, :], start=(h == 0), stop=(h == 1))
                for h in range(2):
                    last_ = nc.tensor.matmul(bp_router_ps, bp_col[:, h:h + 1], router[:, h, :], start=(h == 0), stop=(h == 1))
                last_.then_inc(wp_router_done, 1)

            def mix_biases():
                pe.wait_ge(h_copied, 2 * NT)
                for g in range(2):
                    nc.tensor.matmul(m_const_ps[:, g, :], bv_diag[:, g, :], wp_ext[:, g, :], start=True, stop=False)
                    last_ = nc.tensor.matmul(m_const_ps[:, g, :], head_share[0:1, :], bp_row[0:1, :], start=False, stop=True)
                last_.then_inc(m_const_done, 1)

            HIGH_A, B_CHUNK, LOW_A, B_AND_ONES = range(4)
            passes = [(HIGH_A, w_hi, 0), (HIGH_A, w_lo, 0), (LOW_A, w_hi, 0), (B_CHUNK, w_hi, 1), (B_AND_ONES, w_lo, 1)]

            def transposes(out_, tiles, width):
                for t, tile in enumerate(tiles):
                    last_ = nc.tensor.transpose(out_[0:width, t * P:(t + 1) * P], tile, ident[:, :])
                return last_

            def slot(b, n, m, pair):
                nb = None if b is None else number(b)
                nn = None if n is None else number(n)
                _, products = stages(b, pair)
                nm = None if m is None else number(m)

                def keys(g):
                    for i, (c, w, a) in enumerate(passes):
                        if g == 0 and i == 0:
                            pe.wait_ge(yt_high_done, 3 * nb + 1)
                        if g == 0 and c == LOW_A:
                            pe.wait_ge(yt_low_done, 2 * nb + 1)
                        if g == 0 and c == B_CHUNK:
                            pe.wait_ge(yt_low_done, 2 * nb + 2)
                        if g == 0 and c == B_AND_ONES:
                            pe.wait_ge(yt_high_done, 3 * nb + 3)
                        at = 2 * D + g * CH
                        last_ = nc.tensor.matmul(k_ps[g][0:CH, 0:NT * P], w[:, a, at:at + CH], yt[:, c, :],
                                                 start=(i == 0), stop=(i == len(passes) - 1))
                    last_.then_inc(k_done, 1)

                def queries_and_values(t):
                    for i, (c, w, a) in enumerate(passes):
                        last_ = nc.tensor.matmul(qv_ps[:, t, 0:2 * D], yt[:, c, t * P:(t + 1) * P], w[:, a, 0:2 * D],
                                                 start=(i == 0), stop=(i == len(passes) - 1))
                    last_.then_inc(qv_done, 1)

                def token_transposes(batch):
                    pe.wait_ge(x_loaded[batch[1]], 32 * (batch[0] + 1))
                    for c in range(2):
                        transposes(x_ch_ps[c], [x_tok[batch[1]][:, t, c * CH:(c + 1) * CH] for t in range(NT)],
                                   CH).then_inc(x_ch_done, 1)

                def scores(t):
                    for c in range(2):
                        last_ = nc.tensor.matmul(s_ps[:, t, :], x_ch[:, c, t, 0:P], x_ch[:, c, t, :],
                                                 start=(c == 0), stop=(c == 1))
                    last_.then_inc(s_done, 1)

                def mixed(t):
                    for g in range(2):
                        if t == 0:
                            pe.wait_ge(q_ch_copied, 2 * nb + g + 1)
                            pe.wait_ge(mix_ready, 2 * nb + g + 1)
                        last_ = nc.tensor.matmul(out_ps[:, t, :], q_ch[:, g, t * P:(t + 1) * P], mix[:, g, :],
                                                 start=(g == 0), stop=(g == 1))
                    last_.then_inc(out_done, 1)

                if b is not None:
                    pe.wait_ge(y_twice_done, nb + 1)
                    if is_first(b):
                        pe.wait_ge(const_ready, 1)
                    if b[1] == 0:
                        wait(pe, result_done, 2 * (b[0] - 1) - 1)
                    transposes(yt_ps[0], [y[:, t, 0:A0] for t in range(NT)], P).then_inc(yt_done, 1)
                    if b[1] == 0:
                        wait(pe, result_done, 2 * (b[0] - 1))
                    if n is not None:
                        pe.wait_ge(seg_pt_copied, 2 * (nn + 1))
                    transposes(yt_ps[1], [y[:, t, A0:2 * A0] for t in range(NT)],
                               P).then_inc(yt_done, 1)
                if m is not None and not is_ahead(m):
                    token_transposes(m)
                if is_first(b):
                    pe.wait_ge(wp_ready, 1)
                if n is not None:
                    if b is None:
                        pe.wait_ge(const_built, CONSTANTS)
                    pe.wait_ge(seg_pt_copied, 2 * (nn + 1))
                    pe.wait_ge(x_router_copied, nn + 1)
                    wait(pe, h2_done, 2 * (nn - 1))
                    for t in range(NT):
                        last_ = nc.tensor.matmul(h_ps[:, t, :], seg_pt[:, t, :], x_tok[n[1]][:, t, :], start=True, stop=True)
                    last_.then_inc(h_done, 1)
                if b is not None:
                    keys(0)
                    keys(1)
                    if m is not None:
                        pe.wait_ge(x_ch_copied, 2 * (nm + 1))
                    for t in range(NT):
                        queries_and_values(t)
                if m is not None:
                    if n is None:
                        pe.wait_ge(router_ready, 2)
                    pe.wait_ge(x_ch_copied, 2 * (nm + 1))
                if b is not None:
                    for g in range(2):
                        pe.wait_ge(k_exp_done, 2 * nb + g + 1)
                        for t in range(NT):
                            last_ = nc.tensor.transpose(k_tok_ps[:, t, g, :], k_exp[:, g, t * P:(t + 1) * P],
                                                        ident[0:CH, 0:CH])
                    last_.then_inc(k_tok_done, 1)
                if m is not None:
                    scores(0)
                    scores(1)
                if is_first(b):
                    mix_biases()
                if b is not None:
                    pe.wait_ge(k_tok_copied, nb + 1)
                    for g in range(2):
                        h = slice(g * CH, (g + 1) * CH)
                        for t in range(NT):
                            if g == 0 and t == 0:
                                pe.wait_ge(v_copied, 2 * nb + 1)
                            if g == 0 and t == NT - 1:
                                pe.wait_ge(v_copied, 2 * (nb + 1))
                            last_ = nc.tensor.matmul(kv_ps[:, g, :], v_tok[:, t, h], k_tok[:, t, h],
                                                     start=(t == 0), stop=(t == NT - 1))
                    last_.then_inc(kv_done, 1)
                if m is not None:
                    scores(2)
                if b is not None:
                    pe.wait_ge(kv_masked, nb + 1)
                    for g in range(2):
                        last_ = nc.tensor.matmul(mix_ps[:, g, :], kv[:, g, :], wp_ext[:, g, :], start=True, stop=True)
                    last_.then_inc(mix_done, 1)
                    for g in range(2):
                        pe.wait_ge((q_norm0_done, q_norm1_done)[g], nb + 1)
                        transposes(q_ch_ps[g], [q_norm[:, t, g * CH:(g + 1) * CH] for t in range(NT)], CH).then_inc(q_ch_done, 1)
                if n is None and m is not None:
                    transpose_weights()
                ahead = next_ahead(m)
                if ahead is not None and n is not None:
                    token_transposes(ahead)
                if products is not None:
                    pe.wait_ge(coef_done, pair + 1)
                    for i in range(2):
                        transposes(coef_ps[i], [coef_split[:, i * NT + t, :] for t in range(NT)], P).then_inc(coef_t_done, 1)
                if b is not None:
                    if n is not None:
                        pe.wait_ge(h_copied, NT * (nn + 1))
                    mixed(0)
                if products is not None:
                    if isinstance(pair, int) and pair == 0:
                        pe.wait_ge(const_ready, 2)
                    if b is not None:
                        pe.wait_ge(mix_ready, 2 * (nb + 1))
                    for t in range(2 * NT):
                        if t % NT == 0:
                            pe.wait_ge(coef_t_copied, 2 * pair + t // NT + 1)
                        last_ = nc.tensor.matmul(ffn_ps[:, t, :], coef_t[:, t // NT, t % NT * P:(t % NT + 1) * P], w_out_split[:, :],
                                                 start=True, stop=True)
                    last_.then_inc(ffn_done, 1)
                if b is not None:
                    mixed(1)
                if b is None and n is not None:
                    project_router()
                if m is not None:
                    wait_first(pe, seg_exp_done, nm + 1)
                    for t in range(NT):
                        last_ = nc.tensor.transpose(seg_pt_ps[:, t, :], seg_p[:, t, :], ident[:, :])
                    last_.then_inc(seg_pt_done, 1)
                if ahead is not None and n is None:
                    token_transposes(ahead)
                if b is not None:
                    mixed(2)

            schedule(pe, slot)

    return nc


_INS = ["x", "L0_attn_Wq", "L0_attn_bq", "L0_attn_Wk", "L0_attn_bk", "L0_attn_Wv", "L0_attn_bv", "L0_attn_Wp",
        "L0_attn_bp", "L0_ffn_weights_in", "L0_ffn_weights_out"]


def kernel(**inputs):
    import numpy as _np
    import concourse.bacc as _bacc
    from concourse import mybir as _mybir
    from concourse.bass_utils import run_bass_kernel_spmd as _run

    nc = _bacc.Bacc("TRN2", target_bir_lowering=False, num_devices=1)
    arrays, args = {}, []
    for name in _INS:
        a = _np.ascontiguousarray(inputs[name])
        arrays[f"in_{name}_dram"] = a
        args.append(nc.dram_tensor(f"in_{name}_dram", a.shape, _mybir.dt.from_np(a.dtype), kind="ExternalInput").ap())
    batches, rows, width = inputs["x"].shape
    tokens = -(-rows // 128) * 64
    args.append(nc.dram_tensor("out_0_dram", (batches, tokens, width), _mybir.dt.float32, kind="ExternalOutput").ap())
    audio_tower_kernel(nc, *args)
    r = _run(nc, [arrays], core_ids=[0])
    return r.results[0]["out_0_dram"]
```
